# Optimizing a Trainium2 kernel written in Bass

```python
import numpy as np
import jax
import jax.numpy as jnp

def _softmax(x, axis=-1):
    return jax.nn.softmax(x, axis=axis)

def _gelu(x):
    return jax.nn.gelu(x, approximate=True)

def _silu(x):
    return jax.nn.silu(x)

def _sigmoid(x):
    return jax.nn.sigmoid(x)

def _layernorm(x, axis=-1, eps=1e-05):
    m = jnp.mean(x, axis=axis, keepdims=True)
    v = jnp.var(x, axis=axis, keepdims=True)
    return (x - m) / jnp.sqrt(v + eps)

def _scatter_add(tgt, idx, src, axis=0):
    return tgt.at[idx].add(src)

def _segment_sum(src, seg, n):
    return jax.ops.segment_sum(src, seg, n)
kernel_name = 'mk_macaron_d1_jaxref_r8_2306fb'

def setup_inputs(seed: int=0):
    np.random.seed(seed)
    _w = jnp.asarray

    def _L0_attn_setup():
        import jax, jax.numpy as jnp
        import numpy as np
        NHEADS = 16
        SCALE_BASE = 512.0
        EPS = 1e-05

        def _rotate_every_two(x):
            x1 = x[..., ::2]
            x2 = x[..., 1::2]
            return jnp.stack([-x2, x1], axis=-1).reshape(x.shape)

        def _xpos(x, offset=0):
            B, T, C = x.shape
            dim_scale = (jnp.arange(0, C, 2, dtype=jnp.float32) + 0.4 * C) / (1.4 * C)
            pos = jnp.arange(offset, offset + T, dtype=jnp.float32)
            scale = dim_scale[None, :] ** (pos[:, None] / SCALE_BASE)
            inv_freq = 1.0 / 10000.0 ** (jnp.arange(0, C, 2, dtype=jnp.float32) / C)
            sinusoid = pos[:, None] * inv_freq[None, :]
            sin = jnp.repeat(jnp.sin(sinusoid) * scale, 2, axis=-1)
            cos = jnp.repeat(jnp.cos(sinusoid) * scale, 2, axis=-1)
            return x * cos[None] + _rotate_every_two(x) * sin[None]

        def _decay_mask(H, T, dtype):
            gamma = 1.0 - 2.0 ** (-5.0 - jnp.arange(H, dtype=jnp.float32))
            idx = jnp.arange(T)
            diff = idx[:, None] - idx[None, :]
            exp = jnp.where(diff >= 0, diff, 0).astype(jnp.float32)
            mask = jnp.where(diff[None] >= 0, gamma[:, None, None] ** exp[None], 0.0)
            return (mask.astype(dtype), gamma)
        key = jax.random.key(seed)
        ks = jax.random.split(key, 4)
        B, T, C = (4, 128, 256)
        s = 0.02
        return {'x': jax.random.normal(ks[0], (B, T, C), dtype=jnp.float32), 'w_qkv': jax.random.normal(ks[1], (C, 3 * C), dtype=jnp.float32) * s, 'w_g': jax.random.normal(ks[2], (C, C), dtype=jnp.float32) * s, 'w_proj': jax.random.normal(ks[3], (C, C), dtype=jnp.float32) * s, 'gn_weight': jnp.ones((C,), dtype=jnp.float32), 'gn_bias': jnp.zeros((C,), dtype=jnp.float32)}
    _L0_attn_in = _L0_attn_setup()

    def _L0_ffn_setup():
        import jax, jax.numpy as jnp
        import numpy as np
        B, S, H, I = (1, 64, 256, 768)

        def _quantized_matmul(x, w, scale):
            wq = w.astype(jnp.float8_e4m3fn).astype(x.dtype)
            y = jnp.einsum('bsi,io->bso', x, wq)
            return y * scale
        key = jax.random.key(seed)
        ks = jax.random.split(key, 7)
        return {'x': jax.random.normal(ks[0], (B, S, H), dtype=jnp.float32), 'gate_w': jax.random.normal(ks[1], (H, I), dtype=jnp.float32) * 0.02, 'up_w': jax.random.normal(ks[2], (H, I), dtype=jnp.float32) * 0.02, 'down_w': jax.random.normal(ks[3], (I, H), dtype=jnp.float32) * 0.02, 'gate_scale': jax.random.uniform(ks[4], (I,), dtype=jnp.float32, minval=0.5, maxval=1.5), 'up_scale': jax.random.uniform(ks[5], (I,), dtype=jnp.float32, minval=0.5, maxval=1.5), 'down_scale': jax.random.uniform(ks[6], (H,), dtype=jnp.float32, minval=0.5, maxval=1.5)}
    _L0_ffn_in = _L0_ffn_setup()
    _d = {'L0_attn_x': _L0_attn_in['x'], 'L0_attn_w_qkv': _L0_attn_in['w_qkv'], 'L0_attn_w_g': _L0_attn_in['w_g'], 'L0_attn_w_proj': _L0_attn_in['w_proj'], 'L0_attn_gn_weight': _L0_attn_in['gn_weight'], 'L0_attn_gn_bias': _L0_attn_in['gn_bias'], 'L0_ffn_gate_w': _L0_ffn_in['gate_w'], 'L0_ffn_up_w': _L0_ffn_in['up_w'], 'L0_ffn_down_w': _L0_ffn_in['down_w'], 'L0_ffn_gate_scale': _L0_ffn_in['gate_scale'], 'L0_ffn_up_scale': _L0_ffn_in['up_scale'], 'L0_ffn_down_scale': _L0_ffn_in['down_scale']}
    _x0 = _d['L0_attn_x']
    _d['L0_attn_x'] = jax.random.normal(jax.random.fold_in(jax.random.key(seed), 1), (1, 1024, 256), dtype=_x0.dtype)
    del _x0
    return _d

def reference(L0_attn_x, L0_attn_w_qkv, L0_attn_w_g, L0_attn_w_proj, L0_attn_gn_weight, L0_attn_gn_bias, L0_ffn_gate_w, L0_ffn_up_w, L0_ffn_down_w, L0_ffn_gate_scale, L0_ffn_up_scale, L0_ffn_down_scale):

    def _L0_attn_ref(x, w_qkv, w_g, w_proj, gn_weight, gn_bias):
        import jax, jax.numpy as jnp
        import numpy as np
        NHEADS = 16
        SCALE_BASE = 512.0
        EPS = 1e-05

        def _rotate_every_two(x):
            x1 = x[..., ::2]
            x2 = x[..., 1::2]
            return jnp.stack([-x2, x1], axis=-1).reshape(x.shape)

        def _xpos(x, offset=0):
            B, T, C = x.shape
            dim_scale = (jnp.arange(0, C, 2, dtype=jnp.float32) + 0.4 * C) / (1.4 * C)
            pos = jnp.arange(offset, offset + T, dtype=jnp.float32)
            scale = dim_scale[None, :] ** (pos[:, None] / SCALE_BASE)
            inv_freq = 1.0 / 10000.0 ** (jnp.arange(0, C, 2, dtype=jnp.float32) / C)
            sinusoid = pos[:, None] * inv_freq[None, :]
            sin = jnp.repeat(jnp.sin(sinusoid) * scale, 2, axis=-1)
            cos = jnp.repeat(jnp.cos(sinusoid) * scale, 2, axis=-1)
            return x * cos[None] + _rotate_every_two(x) * sin[None]

        def _decay_mask(H, T, dtype):
            gamma = 1.0 - 2.0 ** (-5.0 - jnp.arange(H, dtype=jnp.float32))
            idx = jnp.arange(T)
            diff = idx[:, None] - idx[None, :]
            exp = jnp.where(diff >= 0, diff, 0).astype(jnp.float32)
            mask = jnp.where(diff[None] >= 0, gamma[:, None, None] ** exp[None], 0.0)
            return (mask.astype(dtype), gamma)
        B, T, C = x.shape
        H = NHEADS
        D = C // H
        qkv = x @ w_qkv
        q, k, v = jnp.split(qkv, 3, axis=-1)
        q = _xpos(q, offset=0)
        k = _xpos(k, offset=0)
        q = q.reshape(B, T, H, D).transpose(0, 2, 1, 3)
        k = k.reshape(B, T, H, D).transpose(0, 2, 1, 3)
        v = v.reshape(B, T, H, D).transpose(0, 2, 1, 3)
        mask, _ = _decay_mask(H, T, x.dtype)
        scores = jnp.einsum('bhtd,bhsd->bhts', q, k) * D ** (-0.5)
        scores = scores * mask[None]
        y = jnp.einsum('bhts,bhsd->bhtd', scores, v)
        yg = y.transpose(0, 2, 1, 3).reshape(B * T, H, D)
        mu = jnp.mean(yg, axis=-1, keepdims=True)
        var = jnp.var(yg, axis=-1, keepdims=True)
        yn = (yg - mu) / jnp.sqrt(var + EPS)
        yn = yn.reshape(B * T, C) * gn_weight[None] + gn_bias[None]
        yn = yn.reshape(B, T, C)
        out = jax.nn.silu(x @ w_g) * yn
        return out @ w_proj

    def _L0_ffn_ref(x, gate_w, up_w, down_w, gate_scale, up_scale, down_scale):
        import jax, jax.numpy as jnp
        import numpy as np
        B, S, H, I = (1, 64, 256, 768)

        def _quantized_matmul(x, w, scale):
            wq = w.astype(jnp.float8_e4m3fn).astype(x.dtype)
            y = jnp.einsum('bsi,io->bso', x, wq)
            return y * scale
        gate = jax.nn.silu(_quantized_matmul(x, gate_w, gate_scale))
        up = _quantized_matmul(x, up_w, up_scale)
        fuse = gate * up
        return _quantized_matmul(fuse, down_w, down_scale)
    x = L0_attn_x
    x = x + 0.5 * _L0_ffn_ref(_layernorm(x, axis=-1), L0_ffn_gate_w, L0_ffn_up_w, L0_ffn_down_w, L0_ffn_gate_scale, L0_ffn_up_scale, L0_ffn_down_scale)
    x = x + _L0_attn_ref(_layernorm(x, axis=-1), L0_attn_w_qkv, L0_attn_w_g, L0_attn_w_proj, L0_attn_gn_weight, L0_attn_gn_bias)
    x = x + 0.5 * _L0_ffn_ref(_layernorm(x, axis=-1), L0_ffn_gate_w, L0_ffn_up_w, L0_ffn_down_w, L0_ffn_gate_scale, L0_ffn_up_scale, L0_ffn_down_scale)
    return x

_drawn_inputs = setup_inputs


def setup_inputs(seed=0):
    import zlib

    import numpy as np

    out = dict(_drawn_inputs(seed))
    spreads = {'L0_attn_gn_weight': (1.0, 0.6), 'L0_attn_gn_bias': (0.0, 0.8)}
    factors = {'L0_ffn_gate_scale': 5.296, 'L0_ffn_up_scale': 6.146, 'L0_ffn_down_scale': 5.964}
    for name, (base, spread) in spreads.items():
        noise = np.random.default_rng([zlib.crc32(name.encode()), seed]).standard_normal(out[name].shape)
        drawn = base * np.exp(spread * noise) if base else spread * noise
        out[name] = jnp.asarray(drawn.astype(out[name].dtype))
    for name, factor in factors.items():
        out[name] = (out[name] * factor).astype(out[name].dtype)
    return out
```

```python
from contextlib import ExitStack

import numpy as np

import concourse.bass as bass
from concourse import mybir

F32, F32R, F16, U32 = mybir.dt.float32, mybir.dt.float32r, mybir.dt.float16, mybir.dt.uint32
ALU = mybir.AluOpType
ACT = mybir.ActivationFunctionType
AX = mybir.AxisListType

P = 128
T, C, I = 1024, 256, 768
H, D = 16, 16
NT = T // P
KC = C // P
NI = I // P
TH = 4
GT = TH * P
NG = NT // TH
HG = 4
EPS = 1e-5

EXP_BITS, HALF_BIT = 0x7F800000, 0x00400000
GRID = 2.0 ** -20
GRID_MIN = 1.5 * 2.0 ** -6
W_SCALE = 144.0
CUTS = [0, 128, 384, 768]
PIECES = [(m, a, b) for a, b in zip(CUTS, CUTS[1:]) for m in ("gate", "up")] + [("down", 0, 3), ("down", 3, 6)]
EARLY = 2


def rotation_tables():
    f = np.float32
    dim_scale = (np.arange(0, C, 2, dtype=f) + f(0.4 * C)) / f(1.4 * C)
    pos = np.arange(T, dtype=f)
    scale = dim_scale[None, :] ** (pos[:, None] / f(512.0))
    inv_freq = f(1.0) / f(10000.0) ** (np.arange(0, C, 2, dtype=f) / f(C))
    angle = pos[:, None] * inv_freq[None, :]
    cos = (np.cos(angle) * scale).astype(np.float64)
    sin = (np.sin(angle) * scale).astype(np.float64)
    head = np.arange(C // 2) * 2 // D
    log_gamma = np.log1p(-(2.0 ** (-5.0 - head)))
    grow = np.exp(pos.astype(np.float64)[:, None] * log_gamma[None, :])
    q, k = grow * D ** -0.5, 1.0 / grow
    return (np.concatenate([cos * q, cos * k], 1).astype(f), np.concatenate([sin * q, sin * k], 1).astype(f))


def masks():
    p = np.arange(P)
    return np.concatenate([
        np.eye(P), p[:, None] <= p[None, :], p[:, None] // D == p[None, :] // D,
        (p[:, None] // D) % HG == np.arange(HG)[None, :],
    ], 1).astype(np.float32)


def macaron(nc, x, w_qkv, w_g, w_proj, gn_w, gn_b, gate_w, up_w, down_w, gate_s, up_s, down_s,
            cos_t, sin_t, mask_t, out):
    with ExitStack() as ctx:
        def sb(name, shape, dt=F32):
            return ctx.enter_context(nc.sbuf_tensor(name, shape, dt))

        def sem(name):
            return ctx.enter_context(nc.semaphore(name))

        xt = sb("xt", [P, NT, C])
        x1 = sb("x1", [P, NT, C])
        raw = sb("raw", [P, 3 * KC * I])
        grid = sb("grid", [P, 2, KC * 384])
        w16 = sb("w16", [P, 2, KC * 384], F16)
        wr = {m: sb(f"{m}_r", [P, KC * I], F32R) for m in ("gate", "up", "down")}
        wqkv = sb("wqkv", [P, KC, 3 * C])
        wg = sb("wg", [P, KC, C])
        wp = sb("wp", [P, KC, C])
        msk = sb("msk", [P, 3 * P + HG])
        rows = sb("rows", [2 * NI + 2 * KC, P])
        vec = sb("vec", [P, 2 * NI + 2 * KC])
        ds = sb("ds", [P, C])
        neg_half = sb("neg_half", [P, H])
        stats = sb("stats", [P, 3 * NT, 6])
        mv = sb("mv", [P, 3 * NT, 2])
        ve = sb("ve", [P, 3 * NT])
        rstd = sb("rstd", [P, 3 * NT])
        h = sb("h", [P, TH, C])
        hhi = sb("hhi", [P, KC, NG, GT], F32R)
        hlo = sb("hlo", [P, KC, NG, GT], F32R)
        gact = sb("gact", [P, 2, GT])
        fuse = sb("fuse", [P, 2, GT])
        fhi = sb("fhi", [P, NG, NI, GT], F32R)
        flo = sb("flo", [P, NG, NI, GT], F32R)
        yd = sb("yd", [P, 2, C])
        h2 = sb("h2", [P, 2, KC, P])
        rc = sb("rc", [P, 2 * C])
        rs = sb("rs", [P, 2 * C])
        rot = sb("rot", [P, 2, 2 * C])
        qT = sb("qT", [P, 2, KC, P])
        kM = sb("kM", [P, 2, HG, KC, P])
        v2 = sb("v2", [P, 2, H, 2 * D])
        sc = sb("sc", [P, 4, HG, P])
        state = sb("state", [P, KC, P])
        yT = sb("yT", [P, 2, KC, P])
        gsum = sb("gsum", [P, H])
        gd = sb("gd", [P, C])
        gsq = sb("gsq", [P, C])
        gvar = sb("gvar", [P, H])
        gve = sb("gve", [P, H])
        grstd = sb("grstd", [P, H])
        gn = sb("gn", [P, C])
        sg = sb("sg", [P, 3, KC, P])
        ga = sb("ga", [P, KC, P])
        go = sb("go", [P, KC, P])

        raws = {m: raw[:, i * KC * I:(i + 1) * KC * I] for i, m in enumerate(("gate", "up", "down"))}
        cos = raw[:, 0:NT * C].rearrange("p (t c) -> p t c", t=NT)
        sin = raw[:, NT * C:2 * NT * C].rearrange("p (t c) -> p t c", t=NT)
        ident, causal, own = msk[:, 0:P], msk[:, P:2 * P], msk[:, 2 * P:3 * P]
        gate_col, up_col = vec[:, 0:NI], vec[:, NI:2 * NI]
        gnw_col, gnb_col = vec[:, 2 * NI:2 * NI + KC], vec[:, 2 * NI + KC:2 * NI + 2 * KC]
        v_own = [v2[:, b].rearrange("p (a e) w -> p a (e w)", e=2).rearrange("p a (u w) -> p a u w", w=D)[:, :, 0::3]
                 for b in range(2)]

        def piece(base, q):
            m, a, b = PIECES[q]
            if m == "down":
                return base[:, a * C:b * C].rearrange("p (k n) -> p k n", k=b - a)
            return base.rearrange("p (k n) -> p k n", k=KC)[:, :, a:b]

        def packed(ring, q):
            m, a, b = PIECES[q]
            k, n = (b - a, C) if m == "down" else (KC, b - a)
            return ring[:, q % 2, 0:k * n].rearrange("p (k n) -> p k n", k=k)

        bank = [ctx.enter_context(nc.psum_tensor(f"bank{i}", [P, 512], F32)) for i in range(8)]
        turn = [bank[0], bank[1]]
        pairs = [(bank[2], bank[3]), (bank[4], bank[5])]
        downs = [bank[6], bank[7]]
        b_turn, b_qk, b_vg, b_sc, b_y = bank[0], bank[1], bank[2], [bank[3], bank[4]], bank[5]
        b_state, b_gn = bank[6], bank[7]

        x_in = [sem(f"x_in{g}") for g in range(NG)]
        mask_in, rows_in, ds_in = sem("mask_in"), sem("rows_in"), sem("ds_in")
        raw_in = [sem(f"raw_in{q}") for q in range(len(PIECES))]
        wqkv_in, wg_in, wp_in, cos_in, sin_in, stored = (
            sem(n) for n in ("wqkv_in", "wg_in", "wp_in", "cos_in", "sin_in", "stored"))
        exp_done, clip_done, added, sub_dve, sub_pool, half_done, w_ready = (
            sem(n) for n in ("exp_done", "clip_done", "added", "sub_dve", "sub_pool", "half_done", "w_ready"))
        vec_turned, vec_done, ds_done, const_done, v_zero = (
            sem(n) for n in ("vec_turned", "vec_done", "ds_done", "const_done", "v_zero"))
        stats_done, aggr_done, ve_done, rstd_done, h_done, turned = (
            sem(n) for n in ("stats_done", "aggr_done", "ve_done", "rstd_done", "h_done", "turned"))
        hhi_done, hlo_done, gate_done, up_done, silu_done, fuse_done, fhi_done, flo_done = (
            sem(n) for n in ("hhi_done", "hlo_done", "gate_done", "up_done", "silu_done", "fuse_done",
                             "fhi_done", "flo_done"))
        down_done, yd_done, x1_done, out_done = (sem(n) for n in ("down_done", "yd_done", "x1_done", "out_done"))
        h2_done, qk_done, rc_done, rs_done, rot_done, vg_done, v_done, sg_done = (
            sem(n) for n in ("h2_done", "qk_done", "rc_done", "rs_done", "rot_done", "vg_done", "v_done", "sg_done"))
        qk_turned, qk_copied, sc_done, sc_masked, y_half, kv_done, state_done = (
            sem(n) for n in ("qk_turned", "qk_copied", "sc_done", "sc_masked", "y_half", "kv_done",
                             "state_done"))
        yT_done, y_turned, gsum_done, gd_done, gsq_done, gvar_done, gve_done, grstd_done, gn_done = (
            sem(n) for n in ("yT_done", "y_turned", "gsum_done", "gd_done", "gsq_done", "gvar_done", "gve_done",
                             "grstd_done", "gn_done"))
        gn_turned, ga_done, go_done, proj_done, x2_done = (
            sem(n) for n in ("gn_turned", "ga_done", "go_done", "proj_done", "x2_done"))

        root_groups = ([(g * TH, (g + 1) * TH) for g in range(NG)] + [(n, n + 1) for n in range(NT, 2 * NT)]
                       + [(2 * NT + g * TH, 2 * NT + (g + 1) * TH) for g in range(NG)])

        def roots_until(n):
            return next(i for i, (a, b) in enumerate(root_groups) if a <= n < b) + 1

        block = ctx.enter_context(nc.Block())

        @block.sync
        def _(sp):
            x_dram = x.rearrange("b (g t p) c -> (b g) p t c", g=NG, p=P)
            out_dram = out.rearrange("b (t p) c -> (b t) p c", p=P)
            w_dram = {"gate": gate_w.rearrange("(k p) n -> p k n", p=P), "up": up_w.rearrange("(k p) n -> p k n", p=P),
                      "down": down_w.rearrange("(k p) n -> p k n", p=P)}

            def load_piece(q):
                m, a, b = PIECES[q]
                src = w_dram[m][:, a:b, :] if m == "down" else w_dram[m][:, :, a:b]
                sp.dma_start(piece(raws[m], q), src).then_inc(raw_in[q], 16)

            sp.dma_start(xt[:, 0:TH, :], x_dram[0]).then_inc(x_in[0], 16)
            load_piece(0)
            load_piece(1)
            sp.dma_start(msk[:, :], mask_t).then_inc(mask_in, 16)
            load_piece(2)
            load_piece(3)
            for src, at, n in ((gate_s, 0, NI), (up_s, NI, NI), (gn_w, 2 * NI, KC), (gn_b, 2 * NI + KC, KC)):
                sp.dma_start(rows[at:at + n, :], src.rearrange("(i p) -> i p", p=P)).then_inc(rows_in, 16)
            sp.dma_start(xt[:, TH:NT, :], x_dram[1]).then_inc(x_in[1], 16)
            for q in range(4, len(PIECES)):
                load_piece(q)
            sp.dma_start(ds[:, :], down_s.partition_broadcast(P)).then_inc(ds_in, 16)
            sp.dma_start(wqkv[:, :, :], w_qkv.rearrange("(k p) n -> p k n", p=P)).then_inc(wqkv_in, 16)
            sp.dma_start(wg[:, :, :], w_g.rearrange("(k p) n -> p k n", p=P)).then_inc(wg_in, 16)
            sp.dma_start(wp[:, :, :], w_proj.rearrange("(k p) n -> p k n", p=P)).then_inc(wp_in, 16)
            sp.wait_ge(sub_dve, EARLY)
            sp.wait_ge(sub_pool, len(PIECES) - EARLY)
            sp.dma_start(cos, cos_t.rearrange("(t p) c -> p t c", p=P)).then_inc(cos_in, 16)
            sp.dma_start(sin, sin_t.rearrange("(t p) c -> p t c", p=P)).then_inc(sin_in, 16)
            for t in range(NT):
                sp.wait_ge(out_done, t + 1)
                sp.dma_start(out_dram[t], xt[:, t, :]).then_inc(stored, 16)
            sp.wait_ge(stored, 16 * NT)

        @block.gpsimd
        def _(pool):
            def subtract(q):
                pool.wait_ge(added, q + 1)
                pool.tensor_tensor(packed(grid, q), piece(raws[PIECES[q][0]], q), packed(grid, q),
                                   ALU.subtract).then_inc(sub_pool, 1)

            def roots(i):
                a, b = root_groups[i]
                pool.wait_ge(aggr_done, b)
                pool.tensor_scalar(ve[:, a:b], mv[:, a:b, 1], EPS, None, ALU.add).then_inc(ve_done, 1)
                pool.wait_ge(ve_done, i + 1)
                pool.tensor_tensor(rstd[:, a:b], ve[:, a:b], neg_half[:, 0:b - a], ALU.pow).then_inc(rstd_done, 1)

            def rotate(c):
                pool.wait_ge(rs_done, c + 1)
                if c >= 2:
                    pool.wait_ge(kv_done, c - 1)
                    pool.wait_ge(qk_turned, c - 1)
                rc2, rs2 = (t[:, :].rearrange("p (i e) -> p i e", e=2) for t in (rc, rs))
                ro = rot[:, c % 2, :].rearrange("p (i e) -> p i e", e=2)
                pool.tensor_tensor(ro[:, :, 0], rc2[:, :, 0], rs2[:, :, 1], ALU.subtract).then_inc(rot_done, 1)
                pool.tensor_tensor(ro[:, :, 1], rc2[:, :, 1], rs2[:, :, 0], ALU.add).then_inc(rot_done, 1)

            def group_roots(c):
                pool.wait_ge(gvar_done, c + 1)
                pool.tensor_scalar(gve[:, :], gvar[:, :], 1.0 / D, EPS, ALU.mult, ALU.add).then_inc(gve_done, 1)
                pool.wait_ge(gve_done, c + 1)
                pool.tensor_tensor(grstd[:, :], gve[:, :], neg_half[:, :], ALU.pow).then_inc(grstd_done, 1)

            pool.memset(neg_half[:, :], -0.5).then_inc(const_done, 1)
            pool.memset(v2[:, :, :, :], 0.0).then_inc(v_zero, 1)
            pool.wait_ge(const_done, 1)
            roots(0)
            subtract(2)
            subtract(3)
            subtract(4)
            roots(1)
            for q in range(5, len(PIECES)):
                subtract(q)
            roots(2)
            roots(3)
            rotate(0)
            for c in range(NT):
                if c + 1 < NT:
                    rotate(c + 1)
                if c >= 1:
                    group_roots(c - 1)
                if c + 2 < NT:
                    roots(NG + c + 2)
            roots(NG + NT)
            group_roots(NT - 1)
            roots(NG + NT + 1)

        @block.scalar
        def _(act):
            def round_half(q):
                m = PIECES[q][0]
                if q < EARLY:
                    act.wait_ge(sub_dve, q + 1)
                else:
                    act.wait_ge(sub_pool, q - EARLY + 1)
                if q >= 2:
                    act.wait_ge(w_ready, q - 1)
                nc.scalar.activation(packed(w16, q), packed(grid, q), ACT.Copy,
                                     scale=W_SCALE / GRID).then_inc(half_done, 1)
                act.wait_ge(half_done, q + 1)
                nc.scalar.activation(piece(wr[m][:, :], q), packed(w16, q), ACT.Copy).then_inc(w_ready, 1)

            def split_h(g, k):
                act.wait_ge(turned, (g if g < NG else g + NG) * TH + TH)
                if g >= NG:
                    act.wait_ge(up_done, NG * NI)
                nc.scalar.activation(hhi[:, k, g % NG, :], turn[k][:, :], ACT.Copy).then_inc(hhi_done, 1)

            def silu(j):
                if j == 0:
                    act.wait_ge(vec_done, 2)
                act.wait_ge(gate_done, j + 1)
                if j >= 2:
                    act.wait_ge(fuse_done, j - 1)
                i = j % NI
                nc.scalar.activation(gact[:, j % 2, :], pairs[j % 2][0][:, :], ACT.Silu,
                                     scale=gate_col[:, i:i + 1]).then_inc(silu_done, 1)

            def split_f(j):
                act.wait_ge(fuse_done, j + 1)
                if j >= NG * NI:
                    act.wait_ge(down_done, NT)
                nc.scalar.activation(fhi[:, j // NI % NG, j % NI, :], fuse[:, j % 2, :], ACT.Copy).then_inc(fhi_done, 1)

            def copy_h2(c):
                act.wait_ge(turned, NT + c + 1)
                if c >= 2:
                    act.wait_ge(vg_done, c - 1)
                nc.scalar.activation(h2[:, c % 2, :, :], b_turn[:, 0:C].rearrange("p (k t) -> p k t", k=KC),
                                     ACT.Copy).then_inc(h2_done, 1)

            def copy_v(c):
                act.wait_ge(vg_done, c + 1)
                if c == 0:
                    act.wait_ge(v_zero, 1)
                if c >= 2:
                    act.wait_ge(kv_done, c - 1)
                    act.wait_ge(y_half, KC * (c - 1))
                nc.scalar.activation(v_own[c % 2], b_vg[:, 0:C].rearrange("p (a e w) -> p a e w", e=2, w=D),
                                     ACT.Copy).then_inc(v_done, 1)
                if c >= 3:
                    act.wait_ge(go_done, c - 2)
                nc.scalar.activation(sg[:, c % 3, :, :], b_vg[:, C:2 * C].rearrange("p (k t) -> p k t", k=KC),
                                     ACT.Silu).then_inc(sg_done, 1)

            def copy_qk(c):
                act.wait_ge(qk_turned, c + 1)
                if c >= 2:
                    act.wait_ge(y_half, KC * (c - 1))
                turned_qk = b_turn[:, :].rearrange("p (a k t) -> p a k t", a=2, k=KC)
                nc.scalar.activation(qT[:, c % 2, :, :], turned_qk[:, 0], ACT.Copy)
                for m in range(HG):
                    last = nc.scalar.activation(kM[:, c % 2, m, :, :], turned_qk[:, 1], ACT.Copy,
                                                scale=msk[:, 3 * P + m:3 * P + m + 1])
                last.then_inc(qk_copied, 1)

            def copy_y(c):
                act.wait_ge(y_half, KC * (c + 1))
                if c >= 2:
                    act.wait_ge(y_turned, c - 1)
                nc.scalar.activation(yT[:, c % 2, :, :], b_y[:, 0:C].rearrange("p (k t) -> p k t", k=KC),
                                     ACT.Copy).then_inc(yT_done, 1)

            def square(c):
                act.wait_ge(gd_done, c + 1)
                if c >= 1:
                    act.wait_ge(gvar_done, c)
                nc.scalar.activation(gsq[:, :], gd[:, :], ACT.Square).then_inc(gsq_done, 1)

            def affine(c):
                act.wait_ge(gn_turned, c + 1)
                if c >= 1:
                    act.wait_ge(go_done, c)
                for k in range(KC):
                    last = nc.scalar.activation(ga[:, k, :], b_gn[:, C + k * P:C + (k + 1) * P], ACT.Identity,
                                                scale=gnw_col[:, k:k + 1], bias=gnb_col[:, k:k + 1])
                last.then_inc(ga_done, 1)

            round_half(0)
            round_half(1)
            split_h(0, 0)
            split_h(0, 1)
            round_half(2)
            round_half(3)
            silu(0)
            round_half(4)
            silu(1)
            split_f(0)
            round_half(5)
            silu(2)
            split_f(1)
            silu(3)
            split_f(2)
            round_half(6)
            silu(4)
            split_f(3)
            split_h(1, 0)
            split_h(1, 1)
            silu(5)
            split_f(4)
            round_half(7)
            for j in range(NI, 2 * NI):
                silu(j)
                split_f(j - 1)
            split_f(2 * NI - 1)
            copy_h2(0)
            copy_v(0)
            copy_qk(0)
            for c in range(NT):
                if c + 1 < NT:
                    copy_h2(c + 1)
                if c >= 2:
                    affine(c - 2)
                if c >= 1:
                    square(c - 1)
                if c + 1 < NT:
                    copy_v(c + 1)
                copy_y(c)
                if c + 1 < NT:
                    copy_qk(c + 1)
            split_h(2, 0)
            split_h(2, 1)
            affine(NT - 2)
            j0 = NG * NI
            silu(j0)
            square(NT - 1)
            silu(j0 + 1)
            split_f(j0)
            silu(j0 + 2)
            split_f(j0 + 1)
            silu(j0 + 3)
            split_f(j0 + 2)
            affine(NT - 1)
            silu(j0 + 4)
            split_f(j0 + 3)
            silu(j0 + 5)
            split_f(j0 + 4)
            split_f(j0 + 5)
            split_h(3, 0)
            split_h(3, 1)
            for j in range(j0 + NI, j0 + 2 * NI):
                silu(j)
                if j > j0 + NI:
                    split_f(j - 1)
            split_f(j0 + 2 * NI - 1)

        @block.vector
        def _(dve):
            def grid_of(q):
                m = PIECES[q][0]
                dve.wait_ge(raw_in[q], 16)
                if q >= 2:
                    dve.wait_ge(half_done, q - 1)
                w, g = piece(raws[m], q), packed(grid, q)
                dve.tensor_scalar(g.bitcast(U32), w.bitcast(U32), EXP_BITS, HALF_BIT,
                                  ALU.bitwise_and, ALU.bitwise_or).then_inc(exp_done, 1)
                dve.wait_ge(exp_done, q + 1)
                dve.tensor_scalar(g, g, GRID_MIN, None, ALU.max).then_inc(clip_done, 1)
                dve.wait_ge(clip_done, q + 1)
                dve.scalar_tensor_tensor(out=w, in0=w, scalar=GRID, in1=g, op0=ALU.mult, op1=ALU.add).then_inc(added, 1)
                if q < EARLY:
                    dve.wait_ge(added, q + 1)
                    dve.tensor_tensor(g, w, g, ALU.subtract).then_inc(sub_dve, 1)

            def norm_stats(a, b):
                for n in range(a, b):
                    if n < NT:
                        dve.wait_ge(x_in[n // TH], 16)
                    elif n < 2 * NT:
                        dve.wait_ge(x1_done, n - NT + 1)
                    else:
                        dve.wait_ge(x2_done, n - 2 * NT + 1)
                    src = xt if n < NT else x1
                    dve.bn_stats(stats[:, n, :], src[:, n % NT, :]).then_inc(stats_done, 1)
                for n in range(a, b):
                    dve.wait_ge(stats_done, n + 1)
                    dve.bn_aggr(mv[:, n, :], stats[:, n, :]).then_inc(aggr_done, 1)

            def norm(a, b):
                for n in range(a, b):
                    dve.wait_ge(rstd_done, roots_until(n))
                    if n >= TH:
                        dve.wait_ge(turned, n - TH + 1)
                    src = xt if n < NT else x1
                    dve.tensor_scalar(h[:, n % TH, :], src[:, n % NT, :], mv[:, n, 0:1], rstd[:, n:n + 1],
                                      ALU.subtract, ALU.mult).then_inc(h_done, 1)

            def rest_h(g, k):
                dve.wait_ge(hhi_done, KC * g + k + 1)
                if g >= NG:
                    dve.wait_ge(up_done, NG * NI)
                dve.tensor_tensor(hlo[:, k, g % NG, :], turn[k][:, :], hhi[:, k, g % NG, :].bitcast(F32),
                                  ALU.subtract).then_inc(hlo_done, 1)

            def fuse_up(j):
                dve.wait_ge(up_done, j + 1)
                dve.wait_ge(silu_done, j + 1)
                if j >= 2:
                    dve.wait_ge(flo_done, j - 1)
                i = j % NI
                dve.scalar_tensor_tensor(out=fuse[:, j % 2, :], in0=pairs[j % 2][1][:, :], scalar=up_col[:, i:i + 1],
                                         in1=gact[:, j % 2, :], op0=ALU.mult, op1=ALU.mult).then_inc(fuse_done, 1)

            def rest_f(j):
                dve.wait_ge(fhi_done, j + 1)
                if j >= NG * NI:
                    dve.wait_ge(down_done, NT)
                at = (j // NI % NG, j % NI)
                dve.tensor_tensor(flo[:, at[0], at[1], :], fuse[:, j % 2, :], fhi[:, at[0], at[1], :].bitcast(F32),
                                  ALU.subtract).then_inc(flo_done, 1)

            def residual(d):
                t = d % NT
                dve.wait_ge(down_done, d + 1)
                dve.wait_ge(ds_done, 1)
                dve.tensor_tensor(yd[:, d % 2, :], downs[d % 2][:, 0:C], ds[:, :], ALU.mult).then_inc(yd_done, 1)
                dve.wait_ge(yd_done, d + 1)
                src, dst, done = (xt, x1, x1_done) if d < NT else (x1, xt, out_done)
                dve.tensor_tensor(dst[:, t, :], yd[:, d % 2, :], src[:, t, :], ALU.add).then_inc(done, 1)

            def rotate_parts(c):
                dve.wait_ge(qk_done, c + 1)
                if c == 0:
                    dve.wait_ge(cos_in, 16)
                    dve.wait_ge(sin_in, 16)
                if c >= 1:
                    dve.wait_ge(rot_done, 2 * c)
                src = b_qk[:, :].rearrange("p (i e) -> p i e", e=2)
                for table, dst, done in ((cos, rc, rc_done), (sin, rs, rs_done)):
                    dve.tensor_tensor(dst[:, :].rearrange("p (i e) -> p i e", e=2), src,
                                      table[:, c, :].unsqueeze(2).to_broadcast([P, C, 2]), ALU.mult).then_inc(done, 1)

            def mask_scores(c, g):
                n = c * HG + g
                dve.wait_ge(sc_done, n + 1)
                if c >= 1:
                    dve.wait_ge(y_half, KC * (c - 1) + g // 2 + 1)
                dve.tensor_tensor(sc[:, g, :, :], b_sc[g % 2][:, :].rearrange("p (m t) -> p m t", m=HG),
                                  causal.unsqueeze(1).to_broadcast([P, HG, P]), ALU.mult).then_inc(sc_masked, 1)

            def copy_state(c):
                dve.wait_ge(kv_done, c + 1)
                dve.wait_ge(y_half, KC * (c + 1))
                dve.tensor_tensor(state[:, :, :], b_state[:, 0:C].rearrange("p (k d) -> p k d", k=KC),
                                  own.unsqueeze(1).to_broadcast([P, KC, P]), ALU.mult).then_inc(state_done, 1)

            def per_head(t):
                return t.rearrange("p (h d) -> p h d", h=H)

            def group_mean(c):
                dve.wait_ge(y_turned, c + 1)
                dve.tensor_reduce(gsum[:, :], per_head(b_gn[:, 0:C]), AX.X, ALU.add).then_inc(gsum_done, 1)
                dve.wait_ge(gsum_done, c + 1)
                if c >= 1:
                    dve.wait_ge(gn_done, c)
                dve.scalar_tensor_tensor(out=per_head(gd[:, :]), in0=gsum[:, :].unsqueeze(2).to_broadcast([P, H, D]),
                                         scalar=-1.0 / D, in1=per_head(b_gn[:, 0:C]),
                                         op0=ALU.mult, op1=ALU.add).then_inc(gd_done, 1)

            def group_var(c):
                dve.wait_ge(gsq_done, c + 1)
                if c >= 1:
                    dve.wait_ge(gve_done, c)
                dve.tensor_reduce(gvar[:, :], per_head(gsq[:, :]), AX.X, ALU.add).then_inc(gvar_done, 1)

            def group_norm(c):
                dve.wait_ge(grstd_done, c + 1)
                if c >= 1:
                    dve.wait_ge(gn_turned, c)
                dve.tensor_tensor(per_head(gn[:, :]), per_head(gd[:, :]),
                                  grstd[:, :].unsqueeze(2).to_broadcast([P, H, D]), ALU.mult).then_inc(gn_done, 1)

            def gated(c):
                dve.wait_ge(ga_done, c + 1)
                dve.wait_ge(sg_done, c + 1)
                if c >= 1:
                    dve.wait_ge(proj_done, c)
                dve.tensor_tensor(go[:, :, :], ga[:, :, :], sg[:, c % 3, :, :], ALU.mult).then_inc(go_done, 1)

            def add_proj(c):
                dve.wait_ge(proj_done, c + 1)
                dve.tensor_tensor(x1[:, c, :], b_gn[:, 0:C], x1[:, c, :], ALU.add).then_inc(x2_done, 1)

            norm_stats(0, 4)
            grid_of(0)
            grid_of(1)
            norm(0, 4)
            grid_of(2)
            grid_of(3)
            dve.wait_ge(vec_turned, 1)
            dve.tensor_scalar(vec[:, 0:2 * NI], bank[7][:, 0:2 * NI], 1.0 / W_SCALE, None, ALU.mult).then_inc(vec_done, 1)
            dve.tensor_copy(vec[:, 2 * NI:], bank[7][:, 2 * NI:2 * NI + 2 * KC]).then_inc(vec_done, 1)
            rest_h(0, 0)
            rest_h(0, 1)
            grid_of(4)
            norm_stats(4, 8)
            dve.wait_ge(vec_done, 2)
            fuse_up(0)
            grid_of(5)
            fuse_up(1)
            rest_f(0)
            norm(4, 8)
            fuse_up(2)
            rest_f(1)
            fuse_up(3)
            rest_f(2)
            grid_of(6)
            fuse_up(4)
            rest_f(3)
            rest_h(1, 0)
            rest_h(1, 1)
            fuse_up(5)
            rest_f(4)
            grid_of(7)
            dve.wait_ge(ds_in, 16)
            dve.tensor_scalar(ds[:, :], ds[:, :], 0.5 / W_SCALE, None, ALU.mult).then_inc(ds_done, 1)
            for j in range(NI, 2 * NI):
                if j >= NI + 3:
                    residual(j - NI - 3)
                fuse_up(j)
                rest_f(j - 1)
            rest_f(2 * NI - 1)
            norm_stats(8, 10)
            norm(8, 10)
            residual(3)
            residual(4)
            rotate_parts(0)
            for d in range(5, NT):
                residual(d)
            for c in range(NT):
                mask_scores(c, 0)
                if c >= 2:
                    gated(c - 2)
                mask_scores(c, 1)
                if c >= 2:
                    add_proj(c - 2)
                if c + 1 < NT:
                    rotate_parts(c + 1)
                if c >= 1:
                    group_mean(c - 1)
                mask_scores(c, 2)
                if c >= 1:
                    group_var(c - 1)
                if c + 2 < NT:
                    norm_stats(NT + c + 2, NT + c + 3)
                elif c == NT - 2:
                    norm_stats(2 * NT, 2 * NT + 2)
                else:
                    norm_stats(2 * NT + 2, 2 * NT + 4)
                mask_scores(c, 3)
                if c >= 1:
                    group_norm(c - 1)
                if c + 2 < NT:
                    norm(NT + c + 2, NT + c + 3)
                if c + 1 < NT:
                    copy_state(c)
            norm(2 * NT, 2 * NT + TH)
            rest_h(2, 0)
            rest_h(2, 1)
            gated(NT - 2)
            add_proj(NT - 2)
            j0 = NG * NI
            group_mean(NT - 1)
            fuse_up(j0)
            group_var(NT - 1)
            fuse_up(j0 + 1)
            rest_f(j0)
            group_norm(NT - 1)
            fuse_up(j0 + 2)
            rest_f(j0 + 1)
            fuse_up(j0 + 3)
            rest_f(j0 + 2)
            gated(NT - 1)
            fuse_up(j0 + 4)
            rest_f(j0 + 3)
            add_proj(NT - 1)
            norm_stats(2 * NT + TH, 3 * NT)
            fuse_up(j0 + 5)
            rest_f(j0 + 4)
            rest_f(j0 + 5)
            norm(2 * NT + TH, 3 * NT)
            residual(NT)
            residual(NT + 1)
            rest_h(3, 0)
            rest_h(3, 1)
            residual(NT + 2)
            residual(NT + 3)
            for j in range(j0 + NI, j0 + 2 * NI):
                fuse_up(j)
                if j > j0 + NI:
                    rest_f(j - 1)
            rest_f(j0 + 2 * NI - 1)
            for d in range(NT + TH, 2 * NT):
                residual(d)

        @block.tensor
        def _(pe):
            def turn_h(g):
                n0 = (g if g < NG else g + NG) * TH
                if g == 1 or g == 3:
                    pe.wait_ge(hlo_done, KC * g)
                if g == 2:
                    pe.wait_ge(qk_copied, NT)
                    pe.wait_ge(rs_done, NT)
                for t in range(TH):
                    pe.wait_ge(h_done, n0 + t + 1)
                    for k in range(KC):
                        mm = pe.transpose(turn[k][:, t * P:(t + 1) * P], h[:, (n0 + t) % TH, k * P:(k + 1) * P], ident)
                    mm.then_inc(turned, 1)

            def gate_up(j):
                g, i = divmod(j, NI)
                if j < NI:
                    pe.wait_ge(w_ready, [2, 4, 4, 6, 6, 6][i])
                if i == 0:
                    pe.wait_ge(hlo_done, KC * (g + 1))
                if j >= 2:
                    pe.wait_ge(silu_done, j - 1)
                    pe.wait_ge(fuse_done, j - 1)
                if j == NG * NI:
                    pe.wait_ge(sg_done, NT)
                    pe.wait_ge(sc_masked, HG * NT)
                    pe.wait_ge(yT_done, NT)
                for m, dst, done in (("gate", pairs[j % 2][0], gate_done), ("up", pairs[j % 2][1], up_done)):
                    for k in range(KC):
                        w = wr[m][:, k * I + i * P:k * I + (i + 1) * P]
                        for half in (hhi, hlo):
                            mm = pe.matmul(dst[:, :], w, half[:, k, g % NG, :],
                                           start=(k == 0 and half is hhi), stop=(k == KC - 1 and half is hlo))
                    mm.then_inc(done, 1)

            def down(d):
                g, t = divmod(d, TH)
                if t == 0:
                    pe.wait_ge(flo_done, NI * (g + 1))
                    pe.wait_ge(w_ready, len(PIECES))
                if d == 1:
                    pe.wait_ge(vec_done, 2)
                if d >= 2:
                    pe.wait_ge(yd_done, d - 1)
                if d == NT:
                    pe.wait_ge(state_done, NT - 1)
                if d == NT + 1:
                    pe.wait_ge(x2_done, NT)
                for i in range(NI):
                    for half in (fhi, flo):
                        mm = pe.matmul(downs[d % 2][:, 0:C], half[:, g % NG, i, t * P:(t + 1) * P],
                                       wr["down"][:, i * C:(i + 1) * C],
                                       start=(i == 0 and half is fhi), stop=(i == NI - 1 and half is flo))
                mm.then_inc(down_done, 1)

            def turn_h2(c):
                pe.wait_ge(h_done, NT + c + 1)
                if c == 0:
                    pe.wait_ge(hlo_done, KC * NG)
                else:
                    pe.wait_ge(qk_copied, c)
                for k in range(KC):
                    mm = pe.transpose(b_turn[:, k * P:(k + 1) * P], h[:, (NT + c) % TH, k * P:(k + 1) * P], ident)
                mm.then_inc(turned, 1)

            def project_qk(c):
                pe.wait_ge(h2_done, c + 1)
                if c == 0:
                    pe.wait_ge(wqkv_in, 16)
                else:
                    pe.wait_ge(rs_done, c)
                for k in range(KC):
                    mm = pe.matmul(b_qk[:, :], h2[:, c % 2, k, :], wqkv[:, k, 0:2 * C], start=(k == 0), stop=(k == KC - 1))
                mm.then_inc(qk_done, 1)

            def project_vg(c):
                if c == 0:
                    pe.wait_ge(wg_in, 16)
                    pe.wait_ge(silu_done, NG * NI)
                else:
                    pe.wait_ge(sg_done, c)
                for k in range(KC):
                    pe.matmul(b_vg[:, 0:C], h2[:, c % 2, k, :], wqkv[:, k, 2 * C:3 * C], start=(k == 0), stop=(k == KC - 1))
                for m in range(KC):
                    for k in range(KC):
                        mm = pe.matmul(b_vg[:, C + m * P:C + (m + 1) * P], wg[:, k, m * P:(m + 1) * P],
                                       h2[:, c % 2, k, :], start=(k == 0), stop=(k == KC - 1))
                mm.then_inc(vg_done, 1)

            def turn_qk(c):
                pe.wait_ge(rot_done, 2 * (c + 1))
                pe.wait_ge(h2_done, c + 1)
                for a in range(2 * KC):
                    mm = pe.transpose(b_turn[:, a * P:(a + 1) * P], rot[:, c % 2, a * P:(a + 1) * P], ident)
                mm.then_inc(qk_turned, 1)

            def scores(c, g):
                n = c * HG + g
                if g == 0:
                    pe.wait_ge(qk_copied, c + 1)
                if n >= 2:
                    pe.wait_ge(sc_masked, n - 1)
                elif n == 0:
                    pe.wait_ge(fuse_done, NG * NI)
                    pe.wait_ge(silu_done, NG * NI)
                k, r = g // 2, 64 * (g % 2)
                for m in range(HG):
                    mm = pe.matmul(b_sc[g % 2][:, m * P:(m + 1) * P], kM[r:r + 64, c % 2, m, k, :],
                                   qT[r:r + 64, c % 2, k, :], start=True, stop=True)
                mm.then_inc(sc_done, 1)

            def values(c, k):
                if k == 0:
                    pe.wait_ge(v_done, c + 1)
                    if c >= 1:
                        pe.wait_ge(yT_done, c)
                if c >= 1:
                    pe.wait_ge(state_done, c)
                    pe.matmul(b_y[:, k * P:(k + 1) * P], state[:, k, :], qT[:, c % 2, k, :], start=True, stop=False,
                              skip_group_check=True)
                for g in (2 * k, 2 * k + 1):
                    pe.wait_ge(sc_masked, c * HG + g + 1)
                    for m in range(HG):
                        hd = g * HG + m
                        r = (hd // 2 % 4) * 2 * D
                        mm = pe.matmul(b_y[r:r + 2 * D, k * P:(k + 1) * P], v2[:, c % 2, hd, :], sc[:, g, m, :],
                                       start=(c == 0 and hd % 2 == 0), stop=(hd % 2 == 1), skip_group_check=True)
                mm.then_inc(y_half, 1)

            def update_state(c):
                if c == 0:
                    pe.wait_ge(yd_done, NT - 1)
                else:
                    pe.wait_ge(state_done, c)
                for k in range(KC):
                    mm = pe.matmul(b_state[:, k * P:(k + 1) * P], rot[:, c % 2, C + k * P:C + (k + 1) * P],
                                   v_own[c % 2][:, 4 * k:4 * k + 4], start=(c == 0 and k == 0), stop=(k == KC - 1),
                                   skip_group_check=True)
                mm.then_inc(kv_done, 1)

            def turn_y(c):
                pe.wait_ge(yT_done, c + 1)
                if c == 0:
                    pe.wait_ge(yd_done, NT)
                else:
                    pe.wait_ge(x2_done, c)
                for k in range(KC):
                    mm = pe.transpose(b_gn[:, k * P:(k + 1) * P], yT[:, c % 2, k, :], ident)
                mm.then_inc(y_turned, 1)

            def turn_gn(c):
                pe.wait_ge(gn_done, c + 1)
                for k in range(KC):
                    mm = pe.transpose(b_gn[:, C + k * P:C + (k + 1) * P], gn[:, k * P:(k + 1) * P], ident)
                mm.then_inc(gn_turned, 1)

            def project_out(c):
                pe.wait_ge(go_done, c + 1)
                if c == 0:
                    pe.wait_ge(wp_in, 16)
                for k in range(KC):
                    mm = pe.matmul(b_gn[:, 0:C], go[:, k, :], wp[:, k, :], start=(k == 0), stop=(k == KC - 1))
                mm.then_inc(proj_done, 1)

            pe.wait_ge(mask_in, 16)
            pe.wait_ge(rows_in, 16 * 4)
            pe.transpose(bank[7][:, 0:2 * NI + 2 * KC], rows[:, :], ident[0:2 * NI + 2 * KC, 0:2 * NI + 2 * KC]).then_inc(vec_turned, 1)
            turn_h(0)
            for j in range(5):
                gate_up(j)
            turn_h(1)
            for j in range(5, 8):
                gate_up(j)
            for j in range(8, 12):
                gate_up(j)
                down(j - 8)
            turn_h2(0)
            down(4)
            project_qk(0)
            down(5)
            project_vg(0)
            down(6)
            down(7)
            turn_qk(0)
            for c in range(NT):
                if c + 1 < NT:
                    turn_h2(c + 1)
                scores(c, 0)
                scores(c, 1)
                if c >= 2:
                    project_out(c - 2)
                if c + 1 < NT:
                    project_qk(c + 1)
                if c >= 1:
                    turn_y(c - 1)
                scores(c, 2)
                values(c, 0)
                if c + 1 < NT:
                    project_vg(c + 1)
                scores(c, 3)
                values(c, 1)
                if c + 1 < NT:
                    update_state(c)
                if c >= 1:
                    turn_gn(c - 1)
                if c + 1 < NT:
                    turn_qk(c + 1)
            turn_h(2)
            project_out(NT - 2)
            j0 = NG * NI
            turn_y(NT - 1)
            gate_up(j0)
            gate_up(j0 + 1)
            gate_up(j0 + 2)
            turn_gn(NT - 1)
            gate_up(j0 + 3)
            project_out(NT - 1)
            gate_up(j0 + 4)
            gate_up(j0 + 5)
            down(NT)
            down(NT + 1)
            turn_h(3)
            down(NT + 2)
            down(NT + 3)
            for j in range(j0 + NI, j0 + 2 * NI):
                gate_up(j)
            for d in range(NT + TH, 2 * NT):
                down(d)


_INS = ["L0_attn_x", "L0_attn_w_qkv", "L0_attn_w_g", "L0_attn_w_proj", "L0_attn_gn_weight", "L0_attn_gn_bias",
        "L0_ffn_gate_w", "L0_ffn_up_w", "L0_ffn_down_w", "L0_ffn_gate_scale", "L0_ffn_up_scale", "L0_ffn_down_scale"]


def kernel(**inputs):
    import concourse.bacc as bacc
    from concourse.bass_utils import run_bass_kernel_spmd

    nc = bacc.Bacc("TRN2", target_bir_lowering=False, num_devices=1)
    cos_t, sin_t = rotation_tables()
    given = {name: np.ascontiguousarray(inputs[name]) for name in _INS}
    given |= {"cos_table": cos_t, "sin_table": sin_t, "masks": masks()}
    arrays, args = {}, []
    for name, a in given.items():
        arrays[f"in_{name}"] = a
        args.append(nc.dram_tensor(f"in_{name}", a.shape, mybir.dt.from_np(a.dtype), kind="ExternalInput").ap())
    out = nc.dram_tensor("out", (1, T, C), F32, kind="ExternalOutput").ap()
    macaron(nc, *args, out)
    r = run_bass_kernel_spmd(nc, [arrays], core_ids=[0])
    return np.asarray(r.results[0]["out"])
```

```python
from contextlib import ExitStack

import numpy as np

import concourse.bass as bass
from concourse import mybir

F32, F32R, F16, U32 = mybir.dt.float32, mybir.dt.float32r, mybir.dt.float16, mybir.dt.uint32
ALU = mybir.AluOpType
ACT = mybir.ActivationFunctionType
AX = mybir.AxisListType

P = 128
T, C, I = 1024, 256, 768
H, D = 16, 16
NT = T // P
KC = C // P
NI = I // P
TH = 4
GT = TH * P
NG = NT // TH
HG = 4
EPS = 1e-5

EXP_BITS, HALF_BIT = 0x7F800000, 0x00400000
GRID = 2.0 ** -20
GRID_MIN = 1.5 * 2.0 ** -6
W_SCALE = 144.0
CUTS = [0, 128, 384, 768]
PIECES = [(m, a, b) for a, b in zip(CUTS, CUTS[1:]) for m in ("gate", "up")] + [("down", 0, 3), ("down", 3, 6)]
SUB_ON_POOL = [2, 4, 6, 7]


def subs(n):
    on_pool = sum(q < n for q in SUB_ON_POOL)
    return n - on_pool, on_pool


REST_ON_POOL = [j for j in range(NG * NI) if j % 2]


def rests(n):
    on_pool = sum(j < n for j in REST_ON_POOL)
    return n - on_pool, on_pool


def rotation_tables():
    f = np.float32
    dim_scale = (np.arange(0, C, 2, dtype=f) + f(0.4 * C)) / f(1.4 * C)
    pos = np.arange(T, dtype=f)
    scale = dim_scale[None, :] ** (pos[:, None] / f(512.0))
    inv_freq = f(1.0) / f(10000.0) ** (np.arange(0, C, 2, dtype=f) / f(C))
    angle = pos[:, None] * inv_freq[None, :]
    cos = (np.cos(angle) * scale).astype(np.float64)
    sin = (np.sin(angle) * scale).astype(np.float64)
    head = np.arange(C // 2) * 2 // D
    log_gamma = np.log1p(-(2.0 ** (-5.0 - head)))
    grow = np.exp(pos.astype(np.float64)[:, None] * log_gamma[None, :])
    q, k = grow * D ** -0.5, 1.0 / grow
    return (np.concatenate([cos * q, cos * k], 1).astype(f), np.concatenate([sin * q, sin * k], 1).astype(f))


def masks():
    p = np.arange(P)
    return np.concatenate([
        np.eye(P), p[:, None] <= p[None, :], p[:, None] // D == p[None, :] // D,
        (p[:, None] // D) % HG == np.arange(HG)[None, :],
    ], 1).astype(np.float32)


def macaron(nc, x, w_qkv, w_g, w_proj, gn_w, gn_b, gate_w, up_w, down_w, gate_s, up_s, down_s,
            cos_t, sin_t, mask_t, out):
    with ExitStack() as ctx:
        def sb(name, shape, dt=F32):
            return ctx.enter_context(nc.sbuf_tensor(name, shape, dt))

        def sem(name):
            return ctx.enter_context(nc.semaphore(name))

        xt = sb("xt", [P, NT, C])
        x1 = sb("x1", [P, NT, C])
        raw = sb("raw", [P, 3 * KC * I])
        grid = sb("grid", [P, 2, KC * 384])
        w16 = sb("w16", [P, 2, KC * 384], F16)
        wr = {m: sb(f"{m}_r", [P, KC * I], F32R) for m in ("gate", "up", "down")}
        wqkv = sb("wqkv", [P, KC, 3 * C])
        wg = sb("wg", [P, KC, C])
        wp = sb("wp", [P, KC, C])
        msk = sb("msk", [P, 3 * P + HG])
        rows = sb("rows", [2 * NI + 2 * KC, P])
        vec = sb("vec", [P, 2 * NI + 2 * KC])
        ds = sb("ds", [P, C])
        neg_half = sb("neg_half", [P, H])
        warm = sb("warm", [P, 1])
        stats = sb("stats", [P, 3 * NT, 6])
        mv = sb("mv", [P, 3 * NT, 2])
        ve = sb("ve", [P, 3 * NT])
        rstd = sb("rstd", [P, 3 * NT])
        h = sb("h", [P, TH, C])
        hhi = sb("hhi", [P, KC, NG, GT], F32R)
        hlo = sb("hlo", [P, KC, NG, GT], F32R)
        gact = sb("gact", [P, 2, GT])
        fuse = sb("fuse", [P, 2, GT])
        fhi = sb("fhi", [P, NG, NI, GT], F32R)
        flo = sb("flo", [P, NG, NI, GT], F32R)
        yd = sb("yd", [P, 2, C])
        h2 = sb("h2", [P, 2, KC, P])
        rc = sb("rc", [P, 2 * C])
        rs = sb("rs", [P, 2 * C])
        rot = sb("rot", [P, 2, 2 * C])
        qT = sb("qT", [P, 2, KC, P])
        kM = sb("kM", [P, 2, HG, KC, P])
        v2 = sb("v2", [P, 2, H, 2 * D])
        sc = sb("sc", [P, 4, HG, P])
        state = sb("state", [P, KC, P])
        yT = sb("yT", [P, 2, KC, P])
        gsum = sb("gsum", [P, H])
        gd = sb("gd", [P, C])
        gsq = sb("gsq", [P, C])
        gvar = sb("gvar", [P, H])
        gve = sb("gve", [P, H])
        grstd = sb("grstd", [P, H])
        gn = sb("gn", [P, C])
        sg = sb("sg", [P, 3, KC, P])
        ga = sb("ga", [P, KC, P])
        go = sb("go", [P, KC, P])

        raws = {m: raw[:, i * KC * I:(i + 1) * KC * I] for i, m in enumerate(("gate", "up", "down"))}
        cos = raw[:, 0:NT * C].rearrange("p (t c) -> p t c", t=NT)
        sin = raw[:, NT * C:2 * NT * C].rearrange("p (t c) -> p t c", t=NT)
        ident, causal, own = msk[:, 0:P], msk[:, P:2 * P], msk[:, 2 * P:3 * P]
        gate_col, up_col = vec[:, 0:NI], vec[:, NI:2 * NI]
        gnw_col, gnb_col = vec[:, 2 * NI:2 * NI + KC], vec[:, 2 * NI + KC:2 * NI + 2 * KC]
        v_own = [v2[:, b].rearrange("p (a e) w -> p a (e w)", e=2).rearrange("p a (u w) -> p a u w", w=D)[:, :, 0::3]
                 for b in range(2)]

        def piece(base, q):
            m, a, b = PIECES[q]
            if m == "down":
                return base[:, a * C:b * C].rearrange("p (k n) -> p k n", k=b - a)
            return base.rearrange("p (k n) -> p k n", k=KC)[:, :, a:b]

        def packed(ring, q):
            m, a, b = PIECES[q]
            k, n = (b - a, C) if m == "down" else (KC, b - a)
            return ring[:, q % 2, 0:k * n].rearrange("p (k n) -> p k n", k=k)

        bank = [ctx.enter_context(nc.psum_tensor(f"bank{i}", [P, 512], F32)) for i in range(8)]
        turn = [(bank[0], bank[1])] * 3 + [(bank[3], bank[4])]
        pairs = [[(bank[2], bank[3]), (bank[4], bank[5])], [(bank[2], bank[6]), (bank[0], bank[1])]]
        downs = [bank[6], bank[7]] * TH + [bank[i] for i in (7, 5, 7, 5, 7, 5, 3, 4)]
        b_turn, b_qk, b_vg, b_sc, b_y = bank[0], bank[1], bank[2], [bank[3], bank[4]], bank[5]
        b_state, b_gn = bank[6], bank[7]
        b_turned_y = [b_gn] * (NT - 1) + [b_sc[0]]

        x_in = [sem(f"x_in{g}") for g in range(NG)]
        mask_in, rows_in, ds_in = sem("mask_in"), sem("rows_in"), sem("ds_in")
        raw_in = [sem(f"raw_in{q}") for q in range(len(PIECES))]
        wqkv_in, wg_in, wp_in, cos_in, sin_in, stored = (
            sem(n) for n in ("wqkv_in", "wg_in", "wp_in", "cos_in", "sin_in", "stored"))
        exp_done, clip_done, added, sub_dve, sub_pool, half_done, w_ready = (
            sem(n) for n in ("exp_done", "clip_done", "added", "sub_dve", "sub_pool", "half_done", "w_ready"))
        vec_turned, vec_done, ds_done, const_done, v_zero = (
            sem(n) for n in ("vec_turned", "vec_done", "ds_done", "const_done", "v_zero"))
        stats_done, aggr_done, ve_done, rstd_done, h_done, turned = (
            sem(n) for n in ("stats_done", "aggr_done", "ve_done", "rstd_done", "h_done", "turned"))
        hhi_done, hlo_done, gate_done, up_done, silu_done, fuse_done, fhi_done, flo_dve = (
            sem(n) for n in ("hhi_done", "hlo_done", "gate_done", "up_done", "silu_done", "fuse_done",
                             "fhi_done", "flo_dve"))
        flo_pool = sem("flo_pool")
        down_done, yd_done, x1_done, out_done = (sem(n) for n in ("down_done", "yd_done", "x1_done", "out_done"))
        h2_done, qk_done, rc_done, rs_done, rot_done, vg_done, v_done, sg_done = (
            sem(n) for n in ("h2_done", "qk_done", "rc_done", "rs_done", "rot_done", "vg_done", "v_done", "sg_done"))
        qk_turned, qk_copied, sc_done, sc_masked, y_half, kv_done, state_done = (
            sem(n) for n in ("qk_turned", "qk_copied", "sc_done", "sc_masked", "y_half", "kv_done",
                             "state_done"))
        yT_done, y_turned, gsum_done, gd_done, gsq_done, gvar_done, gve_done, grstd_done, gn_done = (
            sem(n) for n in ("yT_done", "y_turned", "gsum_done", "gd_done", "gsq_done", "gvar_done", "gve_done",
                             "grstd_done", "gn_done"))
        gn_turned, ga_done, go_done, proj_done, x2_done = (
            sem(n) for n in ("gn_turned", "ga_done", "go_done", "proj_done", "x2_done"))

        root_groups = ([(g * TH, (g + 1) * TH) for g in range(NG)] + [(n, n + 1) for n in range(NT, 2 * NT)]
                       + [(2 * NT, 2 * NT + TH), (2 * NT + TH, 3 * NT - 1), (3 * NT - 1, 3 * NT)])

        def roots_until(n):
            return next(i for i, (a, b) in enumerate(root_groups) if a <= n < b) + 1

        block = ctx.enter_context(nc.Block())

        @block.sync
        def _(sp):
            x_dram = x.rearrange("b (g t p) c -> (b g) p t c", g=NG, p=P)
            out_dram = out.rearrange("b (t p) c -> (b t) p c", p=P)
            w_dram = {"gate": gate_w.rearrange("(k p) n -> p k n", p=P), "up": up_w.rearrange("(k p) n -> p k n", p=P),
                      "down": down_w.rearrange("(k p) n -> p k n", p=P)}

            def load_piece(q):
                m, a, b = PIECES[q]
                src = w_dram[m][:, a:b, :] if m == "down" else w_dram[m][:, :, a:b]
                sp.dma_start(piece(raws[m], q), src).then_inc(raw_in[q], 16)

            sp.dma_start(xt[:, 0:TH, :], x_dram[0]).then_inc(x_in[0], 16)
            load_piece(0)
            load_piece(1)
            sp.dma_start(msk[:, :], mask_t).then_inc(mask_in, 16)
            load_piece(2)
            load_piece(3)
            for src, at, n in ((gate_s, 0, NI), (up_s, NI, NI), (gn_w, 2 * NI, KC), (gn_b, 2 * NI + KC, KC)):
                sp.dma_start(rows[at:at + n, :], src.rearrange("(i p) -> i p", p=P)).then_inc(rows_in, 16)
            sp.dma_start(xt[:, TH:NT, :], x_dram[1]).then_inc(x_in[1], 16)
            for q in range(4, len(PIECES)):
                load_piece(q)
            sp.dma_start(ds[:, :], down_s.partition_broadcast(P)).then_inc(ds_in, 16)
            sp.dma_start(wqkv[:, :, :], w_qkv.rearrange("(k p) n -> p k n", p=P)).then_inc(wqkv_in, 16)
            sp.dma_start(wg[:, :, :], w_g.rearrange("(k p) n -> p k n", p=P)).then_inc(wg_in, 16)
            sp.dma_start(wp[:, :, :], w_proj.rearrange("(k p) n -> p k n", p=P)).then_inc(wp_in, 16)
            sp.wait_ge(sub_dve, subs(len(PIECES))[0])
            sp.wait_ge(sub_pool, subs(len(PIECES))[1])
            sp.dma_start(cos, cos_t.rearrange("(t p) c -> p t c", p=P)).then_inc(cos_in, 16)
            sp.dma_start(sin, sin_t.rearrange("(t p) c -> p t c", p=P)).then_inc(sin_in, 16)
            for t in range(NT):
                sp.wait_ge(out_done, t + 1)
                sp.dma_start(out_dram[t], xt[:, t, :]).then_inc(stored, 16)
            sp.wait_ge(stored, 16 * NT)

        @block.gpsimd
        def _(pool):
            def subtract(q):
                pool.wait_ge(added, q + 1)
                pool.tensor_tensor(packed(grid, q), piece(raws[PIECES[q][0]], q), packed(grid, q),
                                   ALU.subtract).then_inc(sub_pool, 1)

            def roots(i):
                a, b = root_groups[i]
                pool.wait_ge(aggr_done, b)
                pool.tensor_scalar(ve[:, a:b], mv[:, a:b, 1], EPS, None, ALU.add).then_inc(ve_done, 1)
                pool.wait_ge(ve_done, i + 1)
                pool.tensor_tensor(rstd[:, a:b], ve[:, a:b], neg_half[:, 0:b - a], ALU.pow).then_inc(rstd_done, 1)

            def rest_f(j):
                pool.wait_ge(fhi_done, j + 1)
                at = (j // NI % NG, j % NI)
                pool.tensor_tensor(flo[:, at[0], at[1], :], fuse[:, j % 2, :], fhi[:, at[0], at[1], :].bitcast(F32),
                                   ALU.subtract).then_inc(flo_pool, 1)

            def add_down(t):
                pool.wait_ge(yd_done, t + 1)
                pool.tensor_tensor(x1[:, t, :], yd[:, t % 2, :], xt[:, t, :], ALU.add).then_inc(x1_done, 1)

            def group_roots(c):
                pool.wait_ge(gvar_done, c + 1)
                pool.tensor_scalar(gve[:, :], gvar[:, :], 1.0 / D, EPS, ALU.mult, ALU.add).then_inc(gve_done, 1)
                pool.wait_ge(gve_done, c + 1)
                pool.tensor_tensor(grstd[:, :], gve[:, :], neg_half[:, :], ALU.pow).then_inc(grstd_done, 1)

            pool.memset(neg_half[:, :], -0.5).then_inc(const_done, 1)
            pool.memset(v2[:, :, :, :], 0.0).then_inc(v_zero, 1)
            pool.wait_ge(const_done, 1)
            roots(0)
            subtract(2)
            subtract(4)
            roots(1)
            rest_f(1)
            rest_f(3)
            subtract(6)
            rest_f(5)
            subtract(7)
            rest_f(7)
            rest_f(9)
            add_down(0)
            roots(2)
            add_down(1)
            rest_f(11)
            roots(3)
            add_down(2)
            add_down(3)
            for t in range(4, NT):
                add_down(t)
            for c in range(NT):
                if c + 2 < NT:
                    roots(NG + c + 2)
                elif c == NT - 2:
                    roots(NG + NT)
                if c >= 1:
                    group_roots(c - 1)
            group_roots(NT - 1)
            roots(NG + NT + 1)
            roots(NG + NT + 2)

        @block.scalar
        def _(act):
            def round_half(q):
                m = PIECES[q][0]
                if q in SUB_ON_POOL:
                    act.wait_ge(sub_pool, subs(q + 1)[1])
                else:
                    act.wait_ge(sub_dve, subs(q + 1)[0])
                if q >= 2:
                    act.wait_ge(w_ready, q - 1)
                nc.scalar.activation(packed(w16, q), packed(grid, q), ACT.Copy,
                                     scale=W_SCALE / GRID).then_inc(half_done, 1)
                act.wait_ge(half_done, q + 1)
                nc.scalar.activation(piece(wr[m][:, :], q), packed(w16, q), ACT.Copy).then_inc(w_ready, 1)

            def split_h(g, k):
                act.wait_ge(turned, (g if g < NG else g + NG) * TH + TH)
                if g >= NG:
                    act.wait_ge(up_done, NG * NI)
                nc.scalar.activation(hhi[:, k, g % NG, :], turn[g][k][:, :], ACT.Copy).then_inc(hhi_done, 1)

            def silu(j):
                if j == 0:
                    act.wait_ge(vec_done, 2)
                act.wait_ge(gate_done, j + 1)
                if j >= 2:
                    act.wait_ge(fuse_done, j - 1)
                i = j % NI
                nc.scalar.activation(gact[:, j % 2, :], pairs[j // (NG * NI)][j % 2][0][:, :], ACT.Silu,
                                     scale=gate_col[:, i:i + 1]).then_inc(silu_done, 1)

            def split_f(j):
                act.wait_ge(fuse_done, j + 1)
                if j >= NG * NI:
                    act.wait_ge(down_done, NT)
                nc.scalar.activation(fhi[:, j // NI % NG, j % NI, :], fuse[:, j % 2, :], ACT.Copy).then_inc(fhi_done, 1)

            def copy_h2(c):
                act.wait_ge(turned, NT + c + 1)
                if c >= 2:
                    act.wait_ge(vg_done, c - 1)
                nc.scalar.activation(h2[:, c % 2, :, :], b_turn[:, 0:C].rearrange("p (k t) -> p k t", k=KC),
                                     ACT.Copy).then_inc(h2_done, 1)

            def copy_v(c):
                act.wait_ge(vg_done, c + 1)
                if c == 0:
                    act.wait_ge(v_zero, 1)
                if c >= 2:
                    act.wait_ge(kv_done, c - 1)
                    act.wait_ge(y_half, KC * (c - 1))
                nc.scalar.activation(v_own[c % 2], b_vg[:, 0:C].rearrange("p (a e w) -> p a e w", e=2, w=D),
                                     ACT.Copy).then_inc(v_done, 1)
                if c >= 3:
                    act.wait_ge(go_done, c - 2)
                nc.scalar.activation(sg[:, c % 3, :, :], b_vg[:, C:2 * C].rearrange("p (k t) -> p k t", k=KC),
                                     ACT.Silu).then_inc(sg_done, 1)

            def copy_qk(c):
                act.wait_ge(qk_turned, c + 1)
                if c >= 2:
                    act.wait_ge(y_half, KC * (c - 1))
                turned_qk = b_turn[:, :].rearrange("p (a k t) -> p a k t", a=2, k=KC)
                nc.scalar.activation(qT[:, c % 2, :, :], turned_qk[:, 0], ACT.Copy)
                for m in range(HG):
                    last = nc.scalar.activation(kM[:, c % 2, m, :, :], turned_qk[:, 1], ACT.Copy,
                                                scale=msk[:, 3 * P + m:3 * P + m + 1])
                last.then_inc(qk_copied, 1)

            def copy_y(c):
                act.wait_ge(y_half, KC * (c + 1))
                if c >= 2:
                    act.wait_ge(y_turned, c - 1)
                nc.scalar.activation(yT[:, c % 2, :, :], b_y[:, 0:C].rearrange("p (k t) -> p k t", k=KC),
                                     ACT.Copy).then_inc(yT_done, 1)

            def square(c):
                act.wait_ge(gd_done, c + 1)
                if c >= 1:
                    act.wait_ge(gvar_done, c)
                nc.scalar.activation(gsq[:, :], gd[:, :], ACT.Square).then_inc(gsq_done, 1)

            def affine(c):
                act.wait_ge(gn_turned, c + 1)
                if c >= 1:
                    act.wait_ge(go_done, c)
                for k in range(KC):
                    last = nc.scalar.activation(ga[:, k, :], b_gn[:, C + k * P:C + (k + 1) * P], ACT.Identity,
                                                scale=gnw_col[:, k:k + 1], bias=gnb_col[:, k:k + 1])
                last.then_inc(ga_done, 1)

            act.wait_ge(const_done, 1)
            nc.scalar.activation(warm[:, :], neg_half[:, 0:1], ACT.Silu)
            round_half(0)
            round_half(1)
            split_h(0, 0)
            split_h(0, 1)
            round_half(2)
            round_half(3)
            silu(0)
            round_half(4)
            silu(1)
            split_f(0)
            round_half(5)
            silu(2)
            split_f(1)
            silu(3)
            split_f(2)
            split_h(1, 0)
            split_h(1, 1)
            silu(4)
            split_f(3)
            silu(5)
            split_f(4)
            round_half(6)
            silu(6)
            split_f(5)
            silu(7)
            split_f(6)
            round_half(7)
            for j in range(8, 2 * NI):
                silu(j)
                split_f(j - 1)
            split_f(2 * NI - 1)
            copy_h2(0)
            copy_v(0)
            copy_qk(0)
            copy_h2(1)
            for c in range(NT - 1):
                if c >= 1:
                    square(c - 1)
                copy_v(c + 1)
                copy_qk(c + 1)
                if c >= 1:
                    affine(c - 1)
                copy_y(c)
                if c + 2 < NT:
                    copy_h2(c + 2)
            c, j0 = NT - 1, NG * NI
            square(c - 1)
            split_h(2, 0)
            split_h(2, 1)
            copy_y(c)
            silu(j0)
            affine(c - 1)
            square(c)
            split_f(j0)
            silu(j0 + 1)
            split_f(j0 + 1)
            silu(j0 + 2)
            split_f(j0 + 2)
            silu(j0 + 3)
            affine(c)
            split_f(j0 + 3)
            silu(j0 + 4)
            split_f(j0 + 4)
            silu(j0 + 5)
            split_f(j0 + 5)
            split_h(3, 0)
            split_h(3, 1)
            for j in range(j0 + NI, j0 + 2 * NI):
                silu(j)
                if j > j0 + NI:
                    split_f(j - 1)
            split_f(j0 + 2 * NI - 1)

        @block.vector
        def _(dve):
            def grid_of(q):
                m = PIECES[q][0]
                dve.wait_ge(raw_in[q], 16)
                if q >= 2:
                    dve.wait_ge(half_done, q - 1)
                w, g = piece(raws[m], q), packed(grid, q)
                dve.tensor_scalar(g.bitcast(U32), w.bitcast(U32), EXP_BITS, HALF_BIT,
                                  ALU.bitwise_and, ALU.bitwise_or).then_inc(exp_done, 1)
                dve.wait_ge(exp_done, q + 1)
                dve.tensor_scalar(g, g, GRID_MIN, None, ALU.max).then_inc(clip_done, 1)
                dve.wait_ge(clip_done, q + 1)
                dve.scalar_tensor_tensor(out=w, in0=w, scalar=GRID, in1=g, op0=ALU.mult, op1=ALU.add).then_inc(added, 1)
                if q not in SUB_ON_POOL:
                    dve.wait_ge(added, q + 1)
                    dve.tensor_tensor(g, w, g, ALU.subtract).then_inc(sub_dve, 1)

            def norm_stats(a, b):
                for n in range(a, b):
                    if n < NT:
                        dve.wait_ge(x_in[n // TH], 16)
                    elif n < 2 * NT:
                        dve.wait_ge(x1_done, n - NT + 1)
                    else:
                        dve.wait_ge(x2_done, n - 2 * NT + 1)
                    src = xt if n < NT else x1
                    dve.bn_stats(stats[:, n, :], src[:, n % NT, :]).then_inc(stats_done, 1)
                for n in range(a, b):
                    dve.wait_ge(stats_done, n + 1)
                    dve.bn_aggr(mv[:, n, :], stats[:, n, :]).then_inc(aggr_done, 1)

            def norm(a, b):
                for n in range(a, b):
                    dve.wait_ge(rstd_done, roots_until(n))
                    if n >= TH:
                        dve.wait_ge(turned, n - TH + 1)
                    src = xt if n < NT else x1
                    dve.tensor_scalar(h[:, n % TH, :], src[:, n % NT, :], mv[:, n, 0:1], rstd[:, n:n + 1],
                                      ALU.subtract, ALU.mult).then_inc(h_done, 1)

            def rest_h(g, k):
                dve.wait_ge(hhi_done, KC * g + k + 1)
                if g >= NG:
                    dve.wait_ge(up_done, NG * NI)
                dve.tensor_tensor(hlo[:, k, g % NG, :], turn[g][k][:, :], hhi[:, k, g % NG, :].bitcast(F32),
                                  ALU.subtract).then_inc(hlo_done, 1)

            def fuse_up(j):
                dve.wait_ge(up_done, j + 1)
                dve.wait_ge(silu_done, j + 1)
                if j >= 2:
                    if j - 2 in REST_ON_POOL:
                        dve.wait_ge(flo_pool, rests(j - 1)[1])
                    else:
                        dve.wait_ge(flo_dve, rests(j - 1)[0])
                i = j % NI
                dve.scalar_tensor_tensor(out=fuse[:, j % 2, :], in0=pairs[j // (NG * NI)][j % 2][1][:, :], scalar=up_col[:, i:i + 1],
                                         in1=gact[:, j % 2, :], op0=ALU.mult, op1=ALU.mult).then_inc(fuse_done, 1)

            def rest_f(j):
                dve.wait_ge(fhi_done, j + 1)
                if j >= NG * NI:
                    dve.wait_ge(down_done, NT)
                at = (j // NI % NG, j % NI)
                dve.tensor_tensor(flo[:, at[0], at[1], :], fuse[:, j % 2, :], fhi[:, at[0], at[1], :].bitcast(F32),
                                  ALU.subtract).then_inc(flo_dve, 1)

            def scale_down(d):
                dve.wait_ge(down_done, d + 1)
                if d == 0:
                    dve.wait_ge(ds_done, 1)
                if 2 <= d < NT + 2:
                    dve.wait_ge(x1_done, min(d - 1, NT))
                dve.tensor_tensor(yd[:, d % 2, :], downs[d][:, 0:C], ds[:, :], ALU.mult).then_inc(yd_done, 1)

            def add_down(d):
                dve.wait_ge(yd_done, d + 1)
                dve.tensor_tensor(xt[:, d - NT, :], yd[:, d % 2, :], x1[:, d - NT, :], ALU.add).then_inc(out_done, 1)

            def rotate_parts(c):
                dve.wait_ge(qk_done, c + 1)
                if c == 0:
                    dve.wait_ge(cos_in, 16)
                    dve.wait_ge(sin_in, 16)
                if c >= 1:
                    dve.wait_ge(rot_done, 2 * c)
                src = b_qk[:, :].rearrange("p (i e) -> p i e", e=2)
                for table, dst, done in ((cos, rc, rc_done), (sin, rs, rs_done)):
                    dve.tensor_tensor(dst[:, :].rearrange("p (i e) -> p i e", e=2), src,
                                      table[:, c, :].unsqueeze(2).to_broadcast([P, C, 2]), ALU.mult).then_inc(done, 1)

            def rotate(c):
                dve.wait_ge(rc_done, c + 1)
                dve.wait_ge(rs_done, c + 1)
                if c >= 2:
                    dve.wait_ge(kv_done, c - 1)
                    dve.wait_ge(qk_turned, c - 1)
                rc2, rs2 = (t[:, :].rearrange("p (i e) -> p i e", e=2) for t in (rc, rs))
                ro = rot[:, c % 2, :].rearrange("p (i e) -> p i e", e=2)
                dve.tensor_tensor(ro[:, :, 0], rc2[:, :, 0], rs2[:, :, 1], ALU.subtract).then_inc(rot_done, 1)
                dve.tensor_tensor(ro[:, :, 1], rc2[:, :, 1], rs2[:, :, 0], ALU.add).then_inc(rot_done, 1)

            def mask_scores(c, g):
                n = c * HG + g
                dve.wait_ge(sc_done, n + 1)
                if c >= 1:
                    dve.wait_ge(y_half, KC * (c - 1) + g // 2 + 1)
                dve.tensor_tensor(sc[:, g, :, :], b_sc[g % 2][:, :].rearrange("p (m t) -> p m t", m=HG),
                                  causal.unsqueeze(1).to_broadcast([P, HG, P]), ALU.mult).then_inc(sc_masked, 1)

            def copy_state(c):
                dve.wait_ge(kv_done, c + 1)
                dve.wait_ge(y_half, KC * (c + 1))
                dve.tensor_tensor(state[:, :, :], b_state[:, 0:C].rearrange("p (k d) -> p k d", k=KC),
                                  own.unsqueeze(1).to_broadcast([P, KC, P]), ALU.mult).then_inc(state_done, 1)

            def per_head(t):
                return t.rearrange("p (h d) -> p h d", h=H)

            def group_mean(c):
                dve.wait_ge(y_turned, c + 1)
                dve.tensor_reduce(gsum[:, :], per_head(b_turned_y[c][:, 0:C]), AX.X, ALU.add).then_inc(gsum_done, 1)
                dve.wait_ge(gsum_done, c + 1)
                if c >= 1:
                    dve.wait_ge(gn_done, c)
                dve.scalar_tensor_tensor(out=per_head(gd[:, :]), in0=gsum[:, :].unsqueeze(2).to_broadcast([P, H, D]),
                                         scalar=-1.0 / D, in1=per_head(b_turned_y[c][:, 0:C]),
                                         op0=ALU.mult, op1=ALU.add).then_inc(gd_done, 1)

            def group_var(c):
                dve.wait_ge(gsq_done, c + 1)
                if c >= 1:
                    dve.wait_ge(gve_done, c)
                dve.tensor_reduce(gvar[:, :], per_head(gsq[:, :]), AX.X, ALU.add).then_inc(gvar_done, 1)

            def group_norm(c):
                dve.wait_ge(grstd_done, c + 1)
                if c >= 1:
                    dve.wait_ge(gn_turned, c)
                dve.tensor_tensor(per_head(gn[:, :]), per_head(gd[:, :]),
                                  grstd[:, :].unsqueeze(2).to_broadcast([P, H, D]), ALU.mult).then_inc(gn_done, 1)

            def gated(c):
                dve.wait_ge(ga_done, c + 1)
                dve.wait_ge(sg_done, c + 1)
                if c >= 1:
                    dve.wait_ge(proj_done, c)
                dve.tensor_tensor(go[:, :, :], ga[:, :, :], sg[:, c % 3, :, :], ALU.mult).then_inc(go_done, 1)

            def add_proj(c):
                dve.wait_ge(proj_done, c + 1)
                dve.tensor_tensor(x1[:, c, :], b_y[:, C:2 * C], x1[:, c, :], ALU.add).then_inc(x2_done, 1)

            norm_stats(0, 4)
            grid_of(0)
            grid_of(1)
            norm(0, 4)
            grid_of(2)
            rest_h(0, 0)
            rest_h(0, 1)
            grid_of(3)
            dve.wait_ge(vec_turned, 1)
            dve.tensor_scalar(vec[:, 0:2 * NI], bank[7][:, 0:2 * NI], 1.0 / W_SCALE, None, ALU.mult).then_inc(vec_done, 1)
            dve.tensor_copy(vec[:, 2 * NI:], bank[7][:, 2 * NI:2 * NI + 2 * KC]).then_inc(vec_done, 1)
            grid_of(4)
            dve.wait_ge(vec_done, 2)
            grid_of(5)
            fuse_up(0)
            norm_stats(4, 8)
            fuse_up(1)
            rest_f(0)
            norm(4, 8)
            fuse_up(2)
            fuse_up(3)
            rest_f(2)
            rest_h(1, 0)
            rest_h(1, 1)
            fuse_up(4)
            grid_of(6)
            fuse_up(5)
            rest_f(4)
            fuse_up(6)
            grid_of(7)
            dve.wait_ge(ds_in, 16)
            dve.tensor_scalar(ds[:, :], ds[:, :], 0.5 / W_SCALE, None, ALU.mult).then_inc(ds_done, 1)
            fuse_up(7)
            rest_f(6)
            fuse_up(8)
            fuse_up(9)
            rest_f(8)
            scale_down(0)
            fuse_up(10)
            scale_down(1)
            norm_stats(8, 9)
            fuse_up(11)
            rest_f(10)
            norm_stats(9, 10)
            norm(8, 9)
            scale_down(2)
            norm(9, 10)
            scale_down(3)
            rotate_parts(0)
            rotate(0)
            for d in range(4, NT):
                scale_down(d)
            for c in range(NT - 1):
                mask_scores(c, 0)
                if c >= 2:
                    gated(c - 2)
                mask_scores(c, 1)
                if c >= 1:
                    group_mean(c - 1)
                if c + 2 < NT:
                    norm_stats(NT + c + 2, NT + c + 3)
                else:
                    norm_stats(2 * NT + 2, 2 * NT + TH)
                if c >= 1:
                    group_var(c - 1)
                rotate_parts(c + 1)
                rotate(c + 1)
                if c >= 2:
                    add_proj(c - 2)
                mask_scores(c, 2)
                if c + 2 < NT:
                    norm(NT + c + 2, NT + c + 3)
                if c >= 1:
                    group_norm(c - 1)
                mask_scores(c, 3)
                if c == NT - 3:
                    norm_stats(2 * NT, 2 * NT + 2)
                if c == NT - 2:
                    norm(2 * NT, 2 * NT + 2)
                copy_state(c)
            norm(2 * NT + 2, 2 * NT + TH)
            c, j0 = NT - 1, NG * NI
            mask_scores(c, 0)
            gated(c - 2)
            mask_scores(c, 1)
            group_mean(c - 1)
            add_proj(c - 2)
            group_var(c - 1)
            mask_scores(c, 2)
            rest_h(2, 0)
            mask_scores(c, 3)
            rest_h(2, 1)
            group_norm(c - 1)
            norm_stats(2 * NT + TH, 3 * NT - 2)
            group_mean(c)
            fuse_up(j0)
            gated(c - 1)
            group_var(c)
            rest_f(j0)
            fuse_up(j0 + 1)
            add_proj(c - 1)
            norm_stats(3 * NT - 2, 3 * NT - 1)
            rest_f(j0 + 1)
            fuse_up(j0 + 2)
            group_norm(c)
            rest_f(j0 + 2)
            fuse_up(j0 + 3)
            gated(c)
            norm(2 * NT + TH, 3 * NT - 1)
            rest_f(j0 + 3)
            add_proj(c)
            norm_stats(3 * NT - 1, 3 * NT)
            fuse_up(j0 + 4)
            norm(3 * NT - 1, 3 * NT)
            rest_f(j0 + 4)
            fuse_up(j0 + 5)
            rest_f(j0 + 5)
            rest_h(3, 0)
            rest_h(3, 1)
            for d in range(NT, NT + 3):
                scale_down(d)
                add_down(d)
            for i in range(NI):
                fuse_up(j0 + NI + i)
                if i:
                    rest_f(j0 + NI + i - 1)
                if i == 1:
                    scale_down(NT + 3)
                    add_down(NT + 3)
            rest_f(j0 + 2 * NI - 1)
            for d in range(NT + TH, 2 * NT):
                scale_down(d)
                add_down(d)

        @block.tensor
        def _(pe):
            def turn_h(g):
                n0 = (g if g < NG else g + NG) * TH
                if g == 1:
                    pe.wait_ge(hlo_done, KC)
                if g == 2:
                    pe.wait_ge(qk_copied, NT)
                    pe.wait_ge(rs_done, NT)
                if g == 3:
                    pe.wait_ge(sc_masked, HG * NT)
                    pe.wait_ge(gd_done, NT)
                for t in range(TH):
                    pe.wait_ge(h_done, n0 + t + 1)
                    for k in range(KC):
                        mm = pe.transpose(turn[g][k][:, t * P:(t + 1) * P], h[:, (n0 + t) % TH, k * P:(k + 1) * P], ident)
                    mm.then_inc(turned, 1)

            def gate_up(j):
                g, i = divmod(j, NI)
                if j < NI:
                    pe.wait_ge(w_ready, [2, 4, 4, 6, 6, 6][i])
                if i == 0:
                    pe.wait_ge(hhi_done, KC * (g + 1))
                if j >= 2:
                    pe.wait_ge(silu_done, j - 1)
                    pe.wait_ge(fuse_done, j - 1)
                if j == NG * NI:
                    pe.wait_ge(sg_done, NT)
                    pe.wait_ge(state_done, NT - 1)
                for m, dst, done in (("gate", pairs[g // NG][j % 2][0], gate_done), ("up", pairs[g // NG][j % 2][1], up_done)):
                    for half in (hhi, hlo):
                        if half is hlo:
                            pe.wait_ge(hlo_done, KC * (g + 1))
                        for k in range(KC):
                            mm = pe.matmul(dst[:, :], wr[m][:, k * I + i * P:k * I + (i + 1) * P], half[:, k, g % NG, :],
                                           start=(k == 0 and half is hhi), stop=(k == KC - 1 and half is hlo))
                    mm.then_inc(done, 1)

            def down(d, first=0, last=NI):
                g, t = divmod(d, TH)
                n = g * NI + last
                pe.wait_ge(flo_dve, rests(n)[0])
                pe.wait_ge(flo_pool, rests(n)[1])
                if d == 0:
                    pe.wait_ge(w_ready, len(PIECES))
                if first == 0:
                    if d == 1:
                        pe.wait_ge(vec_done, 2)
                    elif 2 <= d < NT or NT + 2 <= d < NT + 6:
                        pe.wait_ge(yd_done, d - 1)
                    elif d == NT:
                        pe.wait_ge(ga_done, NT)
                    elif d == NT + 1:
                        pe.wait_ge(x2_done, NT)
                    elif d >= NT + 6:
                        pe.wait_ge(hlo_done, 2 * NG * KC)
                for i in range(first, last):
                    for half in (fhi, flo):
                        mm = pe.matmul(downs[d][:, 0:C], half[:, g % NG, i, t * P:(t + 1) * P],
                                       wr["down"][:, i * C:(i + 1) * C],
                                       start=(i == 0 and half is fhi), stop=(i == NI - 1 and half is flo))
                if last == NI:
                    mm.then_inc(down_done, 1)

            def turn_h2(c):
                pe.wait_ge(h_done, NT + c + 1)
                if c == 0:
                    pe.wait_ge(hlo_done, KC * NG)
                else:
                    pe.wait_ge(qk_copied, c)
                for k in range(KC):
                    mm = pe.transpose(b_turn[:, k * P:(k + 1) * P], h[:, (NT + c) % TH, k * P:(k + 1) * P], ident)
                mm.then_inc(turned, 1)

            def project_qk(c):
                pe.wait_ge(h2_done, c + 1)
                if c == 0:
                    pe.wait_ge(wqkv_in, 16)
                else:
                    pe.wait_ge(rs_done, c)
                for k in range(KC):
                    mm = pe.matmul(b_qk[:, :], h2[:, c % 2, k, :], wqkv[:, k, 0:2 * C], start=(k == 0), stop=(k == KC - 1))
                mm.then_inc(qk_done, 1)

            def project_vg(c):
                if c == 0:
                    pe.wait_ge(wg_in, 16)
                    pe.wait_ge(silu_done, NG * NI)
                else:
                    pe.wait_ge(sg_done, c)
                for k in range(KC):
                    pe.matmul(b_vg[:, 0:C], h2[:, c % 2, k, :], wqkv[:, k, 2 * C:3 * C], start=(k == 0), stop=(k == KC - 1))
                for m in range(KC):
                    for k in range(KC):
                        mm = pe.matmul(b_vg[:, C + m * P:C + (m + 1) * P], wg[:, k, m * P:(m + 1) * P],
                                       h2[:, c % 2, k, :], start=(k == 0), stop=(k == KC - 1))
                mm.then_inc(vg_done, 1)

            def turn_qk(c):
                pe.wait_ge(rot_done, 2 * (c + 1))
                pe.wait_ge(h2_done, c + 1)
                for a in range(2 * KC):
                    mm = pe.transpose(b_turn[:, a * P:(a + 1) * P], rot[:, c % 2, a * P:(a + 1) * P], ident)
                mm.then_inc(qk_turned, 1)

            def scores(c, g):
                n = c * HG + g
                if g == 0:
                    pe.wait_ge(qk_copied, c + 1)
                if n >= 2:
                    pe.wait_ge(sc_masked, n - 1)
                elif n == 0:
                    pe.wait_ge(fuse_done, NG * NI)
                    pe.wait_ge(silu_done, NG * NI)
                k, r = g // 2, 64 * (g % 2)
                for m in range(HG):
                    mm = pe.matmul(b_sc[g % 2][:, m * P:(m + 1) * P], kM[r:r + 64, c % 2, m, k, :],
                                   qT[r:r + 64, c % 2, k, :], start=True, stop=True)
                mm.then_inc(sc_done, 1)

            def values(c, k):
                if k == 0:
                    pe.wait_ge(v_done, c + 1)
                    if c >= 1:
                        pe.wait_ge(yT_done, c)
                    if c >= 2:
                        pe.wait_ge(x2_done, c - 1)
                if c >= 1:
                    pe.wait_ge(state_done, c)
                    pe.matmul(b_y[:, k * P:(k + 1) * P], state[:, k, :], qT[:, c % 2, k, :], start=True, stop=False,
                              skip_group_check=True)
                for g in (2 * k, 2 * k + 1):
                    pe.wait_ge(sc_masked, c * HG + g + 1)
                    for m in range(HG):
                        hd = g * HG + m
                        r = (hd // 2 % 4) * 2 * D
                        mm = pe.matmul(b_y[r:r + 2 * D, k * P:(k + 1) * P], v2[:, c % 2, hd, :], sc[:, g, m, :],
                                       start=(c == 0 and hd % 2 == 0), stop=(hd % 2 == 1), skip_group_check=True)
                mm.then_inc(y_half, 1)

            def update_state(c):
                if c == 0:
                    pe.wait_ge(yd_done, NT - 1)
                else:
                    pe.wait_ge(state_done, c)
                for k in range(KC):
                    mm = pe.matmul(b_state[:, k * P:(k + 1) * P], rot[:, c % 2, C + k * P:C + (k + 1) * P],
                                   v_own[c % 2][:, 4 * k:4 * k + 4], start=(c == 0 and k == 0), stop=(k == KC - 1),
                                   skip_group_check=True)
                mm.then_inc(kv_done, 1)

            def turn_y(c):
                pe.wait_ge(yT_done, c + 1)
                if c == 0:
                    pe.wait_ge(yd_done, NT)
                elif c == NT - 1:
                    pe.wait_ge(sc_masked, HG * NT - 1)
                else:
                    pe.wait_ge(ga_done, c)
                for k in range(KC):
                    mm = pe.transpose(b_turned_y[c][:, k * P:(k + 1) * P], yT[:, c % 2, k, :], ident)
                mm.then_inc(y_turned, 1)

            def turn_gn(c):
                pe.wait_ge(gn_done, c + 1)
                for k in range(KC):
                    mm = pe.transpose(b_gn[:, C + k * P:C + (k + 1) * P], gn[:, k * P:(k + 1) * P], ident)
                mm.then_inc(gn_turned, 1)

            def project_out(c):
                pe.wait_ge(go_done, c + 1)
                if c == 0:
                    pe.wait_ge(wp_in, 16)
                pe.wait_ge(yT_done, min(c + 2, NT))
                for k in range(KC):
                    mm = pe.matmul(b_y[:, C:2 * C], go[:, k, :], wp[:, k, :], start=(k == 0), stop=(k == KC - 1))
                mm.then_inc(proj_done, 1)

            pe.wait_ge(mask_in, 16)
            pe.wait_ge(rows_in, 16 * 4)
            pe.transpose(bank[7][:, 0:2 * NI + 2 * KC], rows[:, :], ident[0:2 * NI + 2 * KC, 0:2 * NI + 2 * KC]).then_inc(vec_turned, 1)
            turn_h(0)
            for j in range(4):
                gate_up(j)
            turn_h(1)
            for j in range(4, 10):
                gate_up(j)
            down(0)
            gate_up(10)
            down(1)
            gate_up(11)
            down(2)
            down(3)
            turn_h2(0)
            down(4, 0, NI - 1)
            project_qk(0)
            down(4, NI - 1)
            down(5)
            project_vg(0)
            turn_qk(0)
            down(6)
            down(7)
            turn_h2(1)
            for c in range(NT - 1):
                scores(c, 0)
                if c >= 1:
                    turn_y(c - 1)
                scores(c, 1)
                project_qk(c + 1)
                if c >= 2:
                    project_out(c - 2)
                project_vg(c + 1)
                scores(c, 2)
                values(c, 0)
                turn_qk(c + 1)
                scores(c, 3)
                if c >= 1:
                    turn_gn(c - 1)
                values(c, 1)
                update_state(c)
                if c + 2 < NT:
                    turn_h2(c + 2)
            c, j0 = NT - 1, NG * NI
            scores(c, 0)
            scores(c, 1)
            turn_y(c - 1)
            project_out(c - 2)
            turn_h(2)
            scores(c, 2)
            scores(c, 3)
            values(c, 0)
            values(c, 1)
            gate_up(j0)
            turn_y(c)
            turn_gn(c - 1)
            gate_up(j0 + 1)
            project_out(c - 1)
            gate_up(j0 + 2)
            gate_up(j0 + 3)
            turn_gn(c)
            gate_up(j0 + 4)
            project_out(c)
            gate_up(j0 + 5)
            down(NT, 0, NI - 2)
            turn_h(3)
            down(NT + 1, 0, NI - 2)
            down(NT, NI - 2)
            down(NT + 1, NI - 2)
            down(NT + 2)
            gate_up(j0 + NI)
            gate_up(j0 + NI + 1)
            down(NT + 3)
            for j in range(j0 + NI + 2, j0 + 2 * NI):
                gate_up(j)
            d = NT + TH
            down(d, 0, NI - 2)
            for d in range(NT + TH + 1, 2 * NT):
                down(d, 0, NI - 2)
                down(d - 1, NI - 2)
            down(2 * NT - 1, NI - 2)


_INS = ["L0_attn_x", "L0_attn_w_qkv", "L0_attn_w_g", "L0_attn_w_proj", "L0_attn_gn_weight", "L0_attn_gn_bias",
        "L0_ffn_gate_w", "L0_ffn_up_w", "L0_ffn_down_w", "L0_ffn_gate_scale", "L0_ffn_up_scale", "L0_ffn_down_scale"]


def kernel(**inputs):
    import concourse.bacc as bacc
    from concourse.bass_utils import run_bass_kernel_spmd

    nc = bacc.Bacc("TRN2", target_bir_lowering=False, num_devices=1)
    cos_t, sin_t = rotation_tables()
    given = {name: np.ascontiguousarray(inputs[name]) for name in _INS}
    given |= {"cos_table": cos_t, "sin_table": sin_t, "masks": masks()}
    arrays, args = {}, []
    for name, a in given.items():
        arrays[f"in_{name}"] = a
        args.append(nc.dram_tensor(f"in_{name}", a.shape, mybir.dt.from_np(a.dtype), kind="ExternalInput").ap())
    out = nc.dram_tensor("out", (1, T, C), F32, kind="ExternalOutput").ap()
    macaron(nc, *args, out)
    r = run_bass_kernel_spmd(nc, [arrays], core_ids=[0])
    return np.asarray(r.results[0]["out"])
```

```python
from contextlib import ExitStack

import numpy as np

import concourse.bass as bass
from concourse import mybir

F32, F32R, F16, U32 = mybir.dt.float32, mybir.dt.float32r, mybir.dt.float16, mybir.dt.uint32
ALU = mybir.AluOpType
ACT = mybir.ActivationFunctionType
AX = mybir.AxisListType

P = 128
T, C, I = 1024, 256, 768
H, D = 16, 16
NT = T // P
KC = C // P
NI = I // P
TH = 4
GT = TH * P
NG = NT // TH
HG = 4
EPS = 1e-5

EXP_BITS, HALF_BIT = 0x7F800000, 0x00400000
GRID = 2.0 ** -20
GRID_MIN = 1.5 * 2.0 ** -6
W_SCALE = 144.0
CUTS = [0, 128, 384, 768]
PIECES = [(m, a, b) for a, b in zip(CUTS, CUTS[1:]) for m in ("gate", "up")] + [("down", 0, 3), ("down", 3, 6)]
SUB_ON_POOL = [0, 1, 2, 3, 4, 6]


def subs(n):
    on_pool = sum(q < n for q in SUB_ON_POOL)
    return n - on_pool, on_pool


PRODUCTS = ([(g, i) for g in range(NG) for i in range(3)] + [(g, i) for g in range(NG) for i in range(3, NI)]
            + [(g, i) for g in range(NG, 2 * NG) for i in range(NI)])
PIECES_NEEDED = [2, 4, 4, 6, 6, 6]
REST_ON_POOL = [0, 1, 2, 6, 8, 11]
FUSE_SLOTS = 4
WARM_UP = 5


def rests(n):
    on_pool = sum(j < n for j in REST_ON_POOL)
    return n - on_pool, on_pool


def products_until(g, i):
    return PRODUCTS.index((g, i)) + 1


def rotation_table():
    f = np.float32
    dim_scale = (np.arange(0, C, 2, dtype=f) + f(0.4 * C)) / f(1.4 * C)
    pos = np.arange(T, dtype=f)
    scale = dim_scale[None, :] ** (pos[:, None] / f(512.0))
    inv_freq = f(1.0) / f(10000.0) ** (np.arange(0, C, 2, dtype=f) / f(C))
    angle = pos[:, None] * inv_freq[None, :]
    cos = (np.cos(angle) * scale).astype(np.float64)
    sin = (np.sin(angle) * scale).astype(np.float64)
    head = np.arange(C // 2) * 2 // D
    log_gamma = np.log1p(-(2.0 ** (-5.0 - head)))
    grow = np.exp(pos.astype(np.float64)[:, None] * log_gamma[None, :])
    q, k = grow * D ** -0.5, 1.0 / grow
    return np.concatenate([cos * q, cos * k, sin * q, sin * k], 1).astype(f)


def masks():
    p = np.arange(P)
    return np.concatenate([
        np.eye(P), p[:, None] <= p[None, :], p[:, None] // D == p[None, :] // D,
        (p[:, None] // D) % HG == np.arange(HG)[None, :],
    ], 1).astype(np.float32)


def macaron(nc, x, w_qkv, w_g, w_proj, gn_w, gn_b, gate_w, up_w, down_w, gate_s, up_s, down_s,
            rotation_t, mask_t, out):
    with ExitStack() as ctx:
        def sb(name, shape, dt=F32):
            return ctx.enter_context(nc.sbuf_tensor(name, shape, dt))

        def sem(name):
            return ctx.enter_context(nc.semaphore(name))

        xt = sb("xt", [P, NT, C])
        x1 = sb("x1", [P, NT, C])
        raw = sb("raw", [P, 3 * KC * I])
        grid = sb("grid", [P, 2, KC * 384])
        w16 = sb("w16", [P, 2, KC * 384], F16)
        wr = {m: sb(f"{m}_r", [P, KC * I], F32R) for m in ("gate", "up", "down")}
        wqkv = sb("wqkv", [P, KC, 3 * C])
        wg = sb("wg", [P, KC, C])
        wp = sb("wp", [P, KC, C])
        msk = sb("msk", [P, 3 * P + HG])
        rows = sb("rows", [2 * NI + 2 * KC, P])
        vec = sb("vec", [P, 2 * NI + 2 * KC])
        ds = sb("ds", [P, C])
        neg_half = sb("neg_half", [P, H])
        warm = sb("warm", [P, 1])
        stats = sb("stats", [P, 3 * NT, 6])
        mv = sb("mv", [P, 3 * NT, 2])
        ve = sb("ve", [P, 3 * NT])
        rstd = sb("rstd", [P, 3 * NT])
        h = sb("h", [P, TH, C])
        hh = sb("hh", [P, 2, KC, NG, GT], F32R)
        gact = sb("gact", [P, 2, GT])
        fuse = sb("fuse", [P, FUSE_SLOTS, GT])
        fhi = sb("fhi", [P, NG, NI, GT], F32R)
        flo = sb("flo", [P, NG, NI, GT], F32R)
        yd = sb("yd", [P, 2, C])
        h2 = sb("h2", [P, 2, KC, P])
        rc = sb("rc", [P, 2 * C])
        rs = sb("rs", [P, 2 * C])
        rot = sb("rot", [P, 2, 2 * C])
        qT = sb("qT", [P, 2, KC, P])
        rot2 = sb("rot2", [P, 2 * HG, 2, 4 * D], F32R)
        kk = sb("kk", [P, 2, 2, HG, P], F32R)
        v2 = sb("v2", [P, 2, H, 2 * D])
        sc = sb("sc", [P, 4, HG, P])
        state = sb("state", [P, KC, P])
        yT = sb("yT", [P, 2, KC, P])
        gsum = sb("gsum", [P, H])
        gd = sb("gd", [P, 2, C])
        gsq = sb("gsq", [P, C])
        gvar = sb("gvar", [P, H])
        gve = sb("gve", [P, H])
        grstd = sb("grstd", [P, 2, H])
        gn = sb("gn", [P, C])
        sg = sb("sg", [P, 3, KC, P])
        ga = sb("ga", [P, KC, P])
        go = sb("go", [P, KC, P])

        hhi, hlo = hh[:, 0], hh[:, 1]
        qM = [hh[:, :, :, 1, :].rearrange("p a k n -> p (a k) n").rearrange("p g (m t) -> p g m t", m=HG),
              fhi[:, 1, 0:HG, :].rearrange("p g (m t) -> p g m t", m=HG)]

        raws = {m: raw[:, i * KC * I:(i + 1) * KC * I] for i, m in enumerate(("gate", "up", "down"))}
        rotation = raw[:, 0:NT * 2 * C].rearrange("p (t c) -> p t c", t=NT)
        early = 2 * KC * I // (2 * C)
        ident, causal, own = msk[:, 0:P], msk[:, P:2 * P], msk[:, 2 * P:3 * P]
        gate_col, up_col = vec[:, 0:NI], vec[:, NI:2 * NI]
        gnw_col, gnb_col = vec[:, 2 * NI:2 * NI + KC], vec[:, 2 * NI + KC:2 * NI + 2 * KC]
        v_own = [v2[:, b].rearrange("p (a e) w -> p a (e w)", e=2).rearrange("p a (u w) -> p a u w", w=D)[:, :, 0::3]
                 for b in range(2)]

        def piece(base, q):
            m, a, b = PIECES[q]
            if m == "down":
                return base[:, a * C:b * C].rearrange("p (k n) -> p k n", k=b - a)
            return base.rearrange("p (k n) -> p k n", k=KC)[:, :, a:b]

        def packed(ring, q):
            m, a, b = PIECES[q]
            k, n = (b - a, C) if m == "down" else (KC, b - a)
            return ring[:, q % 2, 0:k * n].rearrange("p (k n) -> p k n", k=k)

        bank = [ctx.enter_context(nc.psum_tensor(f"bank{i}", [P, 512], F32)) for i in range(8)]
        turn = [(bank[0], bank[1])] * 3 + [(bank[3], bank[4])]
        pairs = [[(bank[2], bank[3]), (bank[4], bank[5])], [(bank[2], bank[5]), (bank[0], bank[1])]]
        downs = [bank[6], bank[7]] * TH + [bank[i] for i in (6, 7, 6, 7, 6, 7, 3, 4)]
        b_turn, b_qk, b_vg, b_sc, b_y = bank[0], bank[1], bank[2], [bank[3], bank[4]], bank[5]
        b_state, b_gn = bank[6], bank[7]
        b_turned_y = [b_gn] * (NT - 2) + b_sc[::-1]

        x_in = [sem(f"x_in{g}") for g in range(NG)]
        mask_in, rows_in, ds_in = sem("mask_in"), sem("rows_in"), sem("ds_in")
        raw_in = [sem(f"raw_in{q}") for q in range(len(PIECES))]
        wqkv_in, wg_in, wp_in, early_in, late_in, stored = (
            sem(n) for n in ("wqkv_in", "wg_in", "wp_in", "early_in", "late_in", "stored"))
        exp_done, clip_done, added, sub_dve, sub_pool, half_done, w_ready = (
            sem(n) for n in ("exp_done", "clip_done", "added", "sub_dve", "sub_pool", "half_done", "w_ready"))
        vec_turned, vec_done, ds_done, const_done, v_zero = (
            sem(n) for n in ("vec_turned", "vec_done", "ds_done", "const_done", "v_zero"))
        stats_done, aggr_done, ve_done, rstd_done, h_done, turned = (
            sem(n) for n in ("stats_done", "aggr_done", "ve_done", "rstd_done", "h_done", "turned"))
        hhi_done, hlo_done, gate_done, up_done, silu_done, fuse_done, fhi_done, flo_dve = (
            sem(n) for n in ("hhi_done", "hlo_done", "gate_done", "up_done", "silu_done", "fuse_done",
                             "fhi_done", "flo_dve"))
        flo_pool = sem("flo_pool")
        down_done, yd_done, x1_done, out_done = (sem(n) for n in ("down_done", "yd_done", "x1_done", "out_done"))
        h2_done, qk_done, rc_done, rs_done, rot_done, vg_done, v_done, sg_done = (
            sem(n) for n in ("h2_done", "qk_done", "rc_done", "rs_done", "rot_done", "vg_done", "v_done", "sg_done"))
        rhi_done, rlo_done, q_turned, k_turned, q_copied, k_copied, qT_turned, qT_copied = (
            sem(n) for n in ("rhi_done", "rlo_done", "q_turned", "k_turned", "q_copied", "k_copied", "qT_turned",
                             "qT_copied"))
        sc_done, sc_masked, y_half, kv_done, state_done = (
            sem(n) for n in ("sc_done", "sc_masked", "y_half", "kv_done",
                             "state_done"))
        yT_done, y_turned, gsum_done, gd_done, gsq_done, gvar_done, gve_done, grstd_done, gn_done = (
            sem(n) for n in ("yT_done", "y_turned", "gsum_done", "gd_done", "gsq_done", "gvar_done", "gve_done",
                             "grstd_done", "gn_done"))
        gn_turned, ga_done, go_done, proj_done, x2_done = (
            sem(n) for n in ("gn_turned", "ga_done", "go_done", "proj_done", "x2_done"))

        root_groups = ([(g * TH, (g + 1) * TH) for g in range(NG)] + [(n, n + 1) for n in range(NT, 2 * NT)]
                       + [(2 * NT, 2 * NT + TH), (2 * NT + TH, 3 * NT - 1), (3 * NT - 1, 3 * NT)])

        def roots_until(n):
            return next(i for i, (a, b) in enumerate(root_groups) if a <= n < b) + 1

        block = ctx.enter_context(nc.Block())

        @block.sync
        def _(sp):
            x_dram = x.rearrange("b (g t p) c -> (b g) p t c", g=NG, p=P)
            out_dram = out.rearrange("b (t p) c -> (b t) p c", p=P)
            w_dram = {"gate": gate_w.rearrange("(k p) n -> p k n", p=P), "up": up_w.rearrange("(k p) n -> p k n", p=P),
                      "down": down_w.rearrange("(k p) n -> p k n", p=P)}

            def load_piece(q):
                m, a, b = PIECES[q]
                src = w_dram[m][:, a:b, :] if m == "down" else w_dram[m][:, :, a:b]
                sp.dma_start(piece(raws[m], q), src).then_inc(raw_in[q], 16)

            load_piece(0)
            sp.dma_start(xt[:, 0:TH, :], x_dram[0]).then_inc(x_in[0], 16)
            load_piece(1)
            load_piece(2)
            sp.dma_start(msk[:, :], mask_t).then_inc(mask_in, 16)
            for src, at, n in ((gate_s, 0, NI), (up_s, NI, NI), (gn_w, 2 * NI, KC), (gn_b, 2 * NI + KC, KC)):
                sp.dma_start(rows[at:at + n, :], src.rearrange("(i p) -> i p", p=P)).then_inc(rows_in, 16)
            sp.dma_start(xt[:, TH:NT, :], x_dram[1]).then_inc(x_in[1], 16)
            for q in range(3, len(PIECES)):
                load_piece(q)
            sp.dma_start(ds[:, :], down_s.partition_broadcast(P)).then_inc(ds_in, 16)
            sp.dma_start(wqkv[:, :, :], w_qkv.rearrange("(k p) n -> p k n", p=P)).then_inc(wqkv_in, 16)
            sp.dma_start(wg[:, :, :], w_g.rearrange("(k p) n -> p k n", p=P)).then_inc(wg_in, 16)
            sp.dma_start(wp[:, :, :], w_proj.rearrange("(k p) n -> p k n", p=P)).then_inc(wp_in, 16)
            table = rotation_t.rearrange("(t p) c -> p t c", p=P)
            sp.wait_ge(sub_dve, subs(len(PIECES) - 2)[0])
            sp.wait_ge(sub_pool, subs(len(PIECES) - 2)[1])
            sp.dma_start(rotation[:, 0:early, :], table[:, 0:early, :]).then_inc(early_in, 16)
            sp.wait_ge(sub_dve, subs(len(PIECES))[0])
            sp.wait_ge(sub_pool, subs(len(PIECES))[1])
            sp.dma_start(rotation[:, early:NT, :], table[:, early:NT, :]).then_inc(late_in, 16)
            for t in range(NT):
                sp.wait_ge(out_done, t + 1)
                sp.dma_start(out_dram[t], xt[:, t, :]).then_inc(stored, 16)
            sp.wait_ge(stored, 16 * NT)

        @block.gpsimd
        def _(pool):
            def subtract(q):
                pool.wait_ge(added, q + 1)
                pool.tensor_tensor(packed(grid, q), piece(raws[PIECES[q][0]], q), packed(grid, q),
                                   ALU.subtract).then_inc(sub_pool, 1)

            def roots(i):
                a, b = root_groups[i]
                pool.wait_ge(aggr_done, b)
                pool.tensor_scalar(ve[:, a:b], mv[:, a:b, 1], EPS, None, ALU.add).then_inc(ve_done, 1)
                pool.wait_ge(ve_done, i + 1)
                pool.tensor_tensor(rstd[:, a:b], ve[:, a:b], neg_half[:, 0:b - a], ALU.pow).then_inc(rstd_done, 1)

            def rest_f(j):
                pool.wait_ge(fhi_done, j + 1)
                g, i = PRODUCTS[j]
                pool.tensor_tensor(flo[:, g % NG, i, :], fuse[:, j % FUSE_SLOTS, :], fhi[:, g % NG, i, :].bitcast(F32),
                                   ALU.subtract).then_inc(flo_pool, 1)

            def add_down(t):
                pool.wait_ge(yd_done, t + 1)
                pool.tensor_tensor(x1[:, t, :], yd[:, t % 2, :], xt[:, t, :], ALU.add).then_inc(x1_done, 1)

            def group_roots(c):
                pool.wait_ge(gvar_done, c + 1)
                if c >= 1:
                    pool.wait_ge(grstd_done, c)
                pool.tensor_scalar(gve[:, :], gvar[:, :], 1.0 / D, EPS, ALU.mult, ALU.add).then_inc(gve_done, 1)
                pool.wait_ge(gve_done, c + 1)
                if c >= 2:
                    pool.wait_ge(gn_done, c - 1)
                pool.tensor_tensor(grstd[:, c % 2], gve[:, :], neg_half[:, :], ALU.pow).then_inc(grstd_done, 1)

            pool.memset(neg_half[:, :], -0.5).then_inc(const_done, 1)
            pool.memset(v2[:, :, :, :], 0.0).then_inc(v_zero, 1)
            pool.wait_ge(const_done, 1)
            subtract(0)
            roots(0)
            for n in range(1, 4):
                subtract(n)
            roots(1)
            subtract(4)
            for n in range(0, 3):
                rest_f(n)
            subtract(6)
            rest_f(6)
            rest_f(8)
            add_down(0)
            add_down(1)
            roots(2)
            rest_f(11)
            add_down(2)
            add_down(3)
            roots(3)
            roots(4)
            for n in range(4, 8):
                add_down(n)
            for c in range(NT):
                if c + 3 < NT:
                    roots(NG + c + 3)
                elif c == NT - 2:
                    roots(NG + NT)
                if c >= 1:
                    group_roots(c - 1)
            group_roots(NT - 1)
            roots(NG + NT + 1)
            roots(NG + NT + 2)

        @block.scalar
        def _(act):
            def to_half(q):
                if q in SUB_ON_POOL:
                    act.wait_ge(sub_pool, subs(q + 1)[1])
                else:
                    act.wait_ge(sub_dve, subs(q + 1)[0])
                if q >= 2:
                    act.wait_ge(w_ready, q - 1)
                nc.scalar.activation(packed(w16, q), packed(grid, q), ACT.Copy,
                                     scale=W_SCALE / GRID).then_inc(half_done, 1)

            def to_weights(q):
                act.wait_ge(half_done, q + 1)
                nc.scalar.activation(piece(wr[PIECES[q][0]][:, :], q), packed(w16, q), ACT.Copy).then_inc(w_ready, 1)

            def split_h(g, k):
                act.wait_ge(turned, (g if g < NG else g + NG) * TH + TH)
                if g >= NG:
                    act.wait_ge(up_done, NG * NI)
                if g == 2 * NG - 1:
                    act.wait_ge(sc_done, HG * NT)
                nc.scalar.activation(hhi[:, k, g % NG, :], turn[g][k][:, :], ACT.Copy).then_inc(hhi_done, 1)

            def silu(j):
                if j == 0:
                    act.wait_ge(vec_done, 2)
                act.wait_ge(gate_done, j + 1)
                if j >= 2:
                    act.wait_ge(fuse_done, j - 1)
                i = PRODUCTS[j][1]
                nc.scalar.activation(gact[:, j % 2, :], pairs[j // (NG * NI)][j % 2][0][:, :], ACT.Silu,
                                     scale=gate_col[:, i:i + 1]).then_inc(silu_done, 1)

            def split_f(j):
                act.wait_ge(fuse_done, j + 1)
                if j >= NG * NI:
                    act.wait_ge(down_done, NT)
                    if PRODUCTS[j][0] % NG:
                        act.wait_ge(sc_done, HG * NT)
                g, i = PRODUCTS[j]
                nc.scalar.activation(fhi[:, g % NG, i, :], fuse[:, j % FUSE_SLOTS, :], ACT.Copy).then_inc(fhi_done, 1)

            def copy_h2(c):
                act.wait_ge(turned, NT + c + 1)
                if c >= 2:
                    act.wait_ge(qT_turned, c - 1)
                if c >= 2:
                    act.wait_ge(vg_done, c - 1)
                nc.scalar.activation(h2[:, c % 2, :, :], b_turn[:, 0:C].rearrange("p (k t) -> p k t", k=KC),
                                     ACT.Copy).then_inc(h2_done, 1)

            def copy_v(c):
                act.wait_ge(vg_done, c + 1)
                if c == 0:
                    act.wait_ge(v_zero, 1)
                if c >= 2:
                    act.wait_ge(kv_done, c - 1)
                    act.wait_ge(y_half, KC * (c - 1))
                nc.scalar.activation(v_own[c % 2], b_vg[:, 0:C].rearrange("p (a e w) -> p a e w", e=2, w=D),
                                     ACT.Copy).then_inc(v_done, 1)
                if c >= 3:
                    act.wait_ge(go_done, c - 2)
                nc.scalar.activation(sg[:, c % 3, :, :], b_vg[:, C:2 * C].rearrange("p (k t) -> p k t", k=KC),
                                     ACT.Silu).then_inc(sg_done, 1)

            def split_qk(c):
                act.wait_ge(rot_done, 2 * (c + 1))
                if c >= 1:
                    act.wait_ge(q_turned, c)
                nc.scalar.activation(rot2[:, :, 0, :], rot[:, c % 2, :].rearrange("p (g d) -> p g d", d=4 * D),
                                     ACT.Copy).then_inc(rhi_done, 1)

            def copy_q(c):
                act.wait_ge(q_turned, c + 1)
                if c == 0:
                    act.wait_ge(up_done, NG * NI)
                elif c == 1:
                    act.wait_ge(down_done, NT)
                else:
                    act.wait_ge(sc_done, HG * (c - 1))
                for m in range(HG):
                    last = nc.scalar.activation(qM[c % 2][:, :, m, :], b_turn[:, :].rearrange("p (g t) -> p g t", g=HG),
                                                ACT.Copy, scale=msk[:, 3 * P + m:3 * P + m + 1])
                last.then_inc(q_copied, 1)

            def copy_k(c):
                act.wait_ge(k_turned, c + 1)
                if c >= 2:
                    act.wait_ge(sc_done, HG * (c - 1))
                src = b_qk[:, :].rearrange("p (g t) -> p g t", g=HG)
                nc.scalar.activation(kk[:, c % 2, 0], src, ACT.Copy)
                nc.scalar.activation(kk[0:P // 2, c % 2, 1], src[P // 2:P], ACT.Copy)
                nc.scalar.activation(kk[P // 2:P, c % 2, 1], src[0:P // 2], ACT.Copy).then_inc(k_copied, 1)

            def copy_qT(c):
                act.wait_ge(qT_turned, c + 1)
                if c >= 2:
                    act.wait_ge(y_half, KC * (c - 1))
                nc.scalar.activation(qT[:, c % 2, :, :], b_turn[:, C:2 * C].rearrange("p (k t) -> p k t", k=KC),
                                     ACT.Copy).then_inc(qT_copied, 1)

            def copy_y(c):
                act.wait_ge(y_half, KC * (c + 1))
                if c >= 2:
                    act.wait_ge(y_turned, c - 1)
                nc.scalar.activation(yT[:, c % 2, :, :], b_y[:, 0:C].rearrange("p (k t) -> p k t", k=KC),
                                     ACT.Copy).then_inc(yT_done, 1)

            def square(c):
                act.wait_ge(gd_done, c + 1)
                if c >= 1:
                    act.wait_ge(gvar_done, c)
                nc.scalar.activation(gsq[:, :], gd[:, c % 2], ACT.Square).then_inc(gsq_done, 1)

            def affine(c):
                act.wait_ge(gn_turned, c + 1)
                if c >= 1:
                    act.wait_ge(go_done, c)
                for k in range(KC):
                    last = nc.scalar.activation(ga[:, k, :], b_gn[:, C + k * P:C + (k + 1) * P], ACT.Identity,
                                                scale=gnw_col[:, k:k + 1], bias=gnb_col[:, k:k + 1])
                last.then_inc(ga_done, 1)

            act.wait_ge(const_done, 1)
            nc.scalar.activation(warm[:, :], neg_half[:, 0:1], ACT.Silu)
            to_half(0)
            to_weights(0)
            to_half(1)
            to_weights(1)
            to_half(2)
            split_h(0, 0)
            split_h(0, 1)
            to_weights(2)
            to_half(3)
            to_weights(3)
            silu(0)
            silu(1)
            split_h(1, 0)
            split_h(1, 1)
            split_f(0)
            silu(2)
            split_f(1)
            to_half(4)
            silu(3)
            to_weights(4)
            split_f(2)
            to_half(5)
            silu(4)
            to_weights(5)
            silu(5)
            split_f(3)
            split_f(4)
            silu(6)
            split_f(5)
            to_half(6)
            silu(7)
            to_weights(6)
            silu(8)
            for n in range(6, 9):
                split_f(n)
            silu(9)
            to_half(7)
            to_weights(7)
            silu(10)
            split_f(9)
            split_f(10)
            silu(11)
            split_f(11)
            copy_h2(0)
            split_qk(0)
            copy_v(0)
            copy_h2(1)
            copy_k(0)
            copy_q(0)
            for c in range(NT - 1):
                if c + 2 < NT:
                    copy_h2(c + 2)
                copy_qT(c)
                split_qk(c + 1)
                if c >= 2:
                    affine(c - 2)
                copy_k(c + 1)
                copy_q(c + 1)
                copy_v(c + 1)
                if c >= 1:
                    square(c - 1)
                copy_y(c)
            c, j0 = NT - 1, NG * NI
            copy_qT(c)
            split_h(2, 0)
            split_h(2, 1)
            copy_y(c)
            affine(c - 2)
            square(c - 1)
            silu(j0)
            square(c)
            split_f(j0)
            silu(j0 + 1)
            split_f(j0 + 1)
            silu(j0 + 2)
            affine(c - 1)
            split_f(j0 + 2)
            silu(j0 + 3)
            split_f(j0 + 3)
            silu(j0 + 4)
            affine(c)
            split_f(j0 + 4)
            silu(j0 + 5)
            split_f(j0 + 5)
            split_h(3, 0)
            split_h(3, 1)
            for j in range(j0 + NI, j0 + 2 * NI):
                silu(j)
                if j > j0 + NI:
                    split_f(j - 1)
            split_f(j0 + 2 * NI - 1)

        @block.vector
        def _(dve):
            def grid_step(q):
                dve.wait_ge(raw_in[q], 16)
                if q >= 2:
                    dve.wait_ge(half_done, q - 1)
                dve.tensor_scalar(packed(grid, q).bitcast(U32), piece(raws[PIECES[q][0]], q).bitcast(U32),
                                  EXP_BITS, HALF_BIT, ALU.bitwise_and, ALU.bitwise_or).then_inc(exp_done, 1)

            def grid_clip(q):
                dve.wait_ge(exp_done, q + 1)
                dve.tensor_scalar(packed(grid, q), packed(grid, q), GRID_MIN, None, ALU.max).then_inc(clip_done, 1)

            def grid_add(q):
                dve.wait_ge(clip_done, q + 1)
                w = piece(raws[PIECES[q][0]], q)
                dve.scalar_tensor_tensor(out=w, in0=w, scalar=GRID, in1=packed(grid, q),
                                         op0=ALU.mult, op1=ALU.add).then_inc(added, 1)

            def subtract(q):
                dve.wait_ge(added, q + 1)
                dve.tensor_tensor(packed(grid, q), piece(raws[PIECES[q][0]], q), packed(grid, q),
                                  ALU.subtract).then_inc(sub_dve, 1)

            def tile_stats(n):
                if n < NT:
                    dve.wait_ge(x_in[n // TH], 16)
                elif n < 2 * NT:
                    dve.wait_ge(x1_done, n - NT + 1)
                else:
                    dve.wait_ge(x2_done, n - 2 * NT + 1)
                src = xt if n < NT else x1
                dve.bn_stats(stats[:, n, :], src[:, n % NT, :]).then_inc(stats_done, 1)

            def mean_var(n):
                dve.wait_ge(stats_done, n + 1)
                dve.bn_aggr(mv[:, n, :], stats[:, n, :]).then_inc(aggr_done, 1)

            def norm_stats(a, b):
                for n in range(a, b):
                    tile_stats(n)
                for n in range(a, b):
                    mean_var(n)

            def turned_vectors():
                dve.wait_ge(vec_turned, 1)
                dve.tensor_scalar(vec[:, 0:2 * NI], bank[7][:, 0:2 * NI], 1.0 / W_SCALE, None, ALU.mult).then_inc(vec_done, 1)
                dve.tensor_copy(vec[:, 2 * NI:], bank[7][:, 2 * NI:2 * NI + 2 * KC]).then_inc(vec_done, 1)

            def half_scale():
                dve.wait_ge(ds_in, 16)
                dve.tensor_scalar(ds[:, :], ds[:, :], 0.5 / W_SCALE, None, ALU.mult).then_inc(ds_done, 1)

            def norm_tile(n):
                dve.wait_ge(rstd_done, roots_until(n))
                if n >= TH:
                    dve.wait_ge(turned, n - TH + 1)
                src = xt if n < NT else x1
                dve.tensor_scalar(h[:, n % TH, :], src[:, n % NT, :], mv[:, n, 0:1], rstd[:, n:n + 1],
                                  ALU.subtract, ALU.mult).then_inc(h_done, 1)

            def norm(a, b):
                for n in range(a, b):
                    norm_tile(n)

            def rest_h(g, k):
                dve.wait_ge(hhi_done, KC * g + k + 1)
                if g >= NG:
                    dve.wait_ge(up_done, NG * NI)
                if g == 2 * NG - 1:
                    dve.wait_ge(sc_done, HG * NT)
                dve.tensor_tensor(hlo[:, k, g % NG, :], turn[g][k][:, :], hhi[:, k, g % NG, :].bitcast(F32),
                                  ALU.subtract).then_inc(hlo_done, 1)

            def fuse_up(j):
                dve.wait_ge(up_done, j + 1)
                dve.wait_ge(silu_done, j + 1)
                if j == 0:
                    dve.wait_ge(vec_done, 2)
                last = j - FUSE_SLOTS
                if last >= 0:
                    if last in REST_ON_POOL:
                        dve.wait_ge(flo_pool, rests(last + 1)[1])
                    else:
                        dve.wait_ge(flo_dve, rests(last + 1)[0])
                i = PRODUCTS[j][1]
                dve.scalar_tensor_tensor(out=fuse[:, j % FUSE_SLOTS, :], in0=pairs[j // (NG * NI)][j % 2][1][:, :], scalar=up_col[:, i:i + 1],
                                         in1=gact[:, j % 2, :], op0=ALU.mult, op1=ALU.mult).then_inc(fuse_done, 1)

            def rest_f(j):
                dve.wait_ge(fhi_done, j + 1)
                if j >= NG * NI:
                    dve.wait_ge(down_done, NT)
                g, i = PRODUCTS[j]
                dve.tensor_tensor(flo[:, g % NG, i, :], fuse[:, j % FUSE_SLOTS, :], fhi[:, g % NG, i, :].bitcast(F32),
                                  ALU.subtract).then_inc(flo_dve, 1)

            def scale_down(d):
                dve.wait_ge(down_done, d + 1)
                if d == 0:
                    dve.wait_ge(ds_done, 1)
                if 2 <= d < NT + 2:
                    dve.wait_ge(x1_done, min(d - 1, NT))
                dve.tensor_tensor(yd[:, d % 2, :], downs[d][:, 0:C], ds[:, :], ALU.mult).then_inc(yd_done, 1)

            def add_down(d):
                dve.wait_ge(yd_done, d + 1)
                dve.tensor_tensor(xt[:, d - NT, :], yd[:, d % 2, :], x1[:, d - NT, :], ALU.add).then_inc(out_done, 1)

            def rotate_parts(c):
                dve.wait_ge(qk_done, c + 1)
                if c == 0:
                    dve.wait_ge(early_in, 16)
                if c == early:
                    dve.wait_ge(late_in, 16)
                if c >= 1:
                    dve.wait_ge(rot_done, 2 * c)
                src = b_qk[:, :].rearrange("p (i e) -> p i e", e=2)
                for a, dst, done in ((0, rc, rc_done), (C, rs, rs_done)):
                    dve.tensor_tensor(dst[:, :].rearrange("p (i e) -> p i e", e=2), src,
                                      rotation[:, c, a:a + C].unsqueeze(2).to_broadcast([P, C, 2]), ALU.mult).then_inc(done, 1)

            def rotate(c):
                dve.wait_ge(rc_done, c + 1)
                dve.wait_ge(rs_done, c + 1)
                if c >= 2:
                    dve.wait_ge(kv_done, c - 1)
                    dve.wait_ge(qT_turned, c - 1)
                rc2, rs2 = (t[:, :].rearrange("p (i e) -> p i e", e=2) for t in (rc, rs))
                ro = rot[:, c % 2, :].rearrange("p (i e) -> p i e", e=2)
                dve.tensor_tensor(ro[:, :, 0], rc2[:, :, 0], rs2[:, :, 1], ALU.subtract).then_inc(rot_done, 1)
                dve.tensor_tensor(ro[:, :, 1], rc2[:, :, 1], rs2[:, :, 0], ALU.add).then_inc(rot_done, 1)

            def rest_qk(c):
                dve.wait_ge(rhi_done, c + 1)
                if c >= 1:
                    dve.wait_ge(q_turned, c)
                dve.tensor_tensor(rot2[:, :, 1, :], rot[:, c % 2, :].rearrange("p (g d) -> p g d", d=4 * D),
                                  rot2[:, :, 0, :].bitcast(F32), ALU.subtract).then_inc(rlo_done, 1)

            def mask_scores(c, g):
                n = c * HG + g
                dve.wait_ge(sc_done, n + 1)
                if c >= 1:
                    dve.wait_ge(y_half, KC * (c - 1) + g // 2 + 1)
                dve.tensor_tensor(sc[:, g, :, :], b_sc[g % 2][:, :].rearrange("p (m t) -> p m t", m=HG),
                                  causal.unsqueeze(1).to_broadcast([P, HG, P]), ALU.mult).then_inc(sc_masked, 1)

            def copy_state(c):
                dve.wait_ge(kv_done, c + 1)
                dve.wait_ge(y_half, KC * (c + 1))
                dve.tensor_tensor(state[:, :, :], b_state[:, 0:C].rearrange("p (k d) -> p k d", k=KC),
                                  own.unsqueeze(1).to_broadcast([P, KC, P]), ALU.mult).then_inc(state_done, 1)

            def per_head(t):
                return t.rearrange("p (h d) -> p h d", h=H)

            def group_mean(c):
                dve.wait_ge(y_turned, c + 1)
                if c >= 1:
                    dve.wait_ge(gd_done, c)
                dve.tensor_reduce(gsum[:, :], per_head(b_turned_y[c][:, 0:C]), AX.X, ALU.add).then_inc(gsum_done, 1)
                dve.wait_ge(gsum_done, c + 1)
                if c >= 2:
                    dve.wait_ge(gn_done, c - 1)
                dve.scalar_tensor_tensor(out=per_head(gd[:, c % 2]), in0=gsum[:, :].unsqueeze(2).to_broadcast([P, H, D]),
                                         scalar=-1.0 / D, in1=per_head(b_turned_y[c][:, 0:C]),
                                         op0=ALU.mult, op1=ALU.add).then_inc(gd_done, 1)

            def group_var(c):
                dve.wait_ge(gsq_done, c + 1)
                if c >= 1:
                    dve.wait_ge(gve_done, c)
                dve.tensor_reduce(gvar[:, :], per_head(gsq[:, :]), AX.X, ALU.add).then_inc(gvar_done, 1)

            def group_norm(c):
                dve.wait_ge(grstd_done, c + 1)
                if c >= 1:
                    dve.wait_ge(gn_turned, c)
                dve.tensor_tensor(per_head(gn[:, :]), per_head(gd[:, c % 2]),
                                  grstd[:, c % 2].unsqueeze(2).to_broadcast([P, H, D]), ALU.mult).then_inc(gn_done, 1)

            def gated(c):
                dve.wait_ge(ga_done, c + 1)
                dve.wait_ge(sg_done, c + 1)
                if c >= 1:
                    dve.wait_ge(proj_done, c)
                dve.tensor_tensor(go[:, :, :], ga[:, :, :], sg[:, c % 3, :, :], ALU.mult).then_inc(go_done, 1)

            def add_proj(c):
                dve.wait_ge(proj_done, c + 1)
                dve.tensor_tensor(x1[:, c, :], b_gn[:, C:2 * C], x1[:, c, :], ALU.add).then_inc(x2_done, 1)

            grid_step(0)
            grid_clip(0)
            grid_add(0)
            tile_stats(0)
            tile_stats(1)
            mean_var(0)
            tile_stats(2)
            mean_var(1)
            tile_stats(3)
            mean_var(2)
            grid_step(1)
            mean_var(3)
            grid_step(2)
            grid_clip(1)
            grid_clip(2)
            grid_add(1)
            grid_add(2)
            for n in range(0, 4):
                norm_tile(n)
            tile_stats(4)
            turned_vectors()
            mean_var(4)
            grid_step(3)
            tile_stats(5)
            grid_clip(3)
            rest_h(0, 0)
            grid_add(3)
            tile_stats(6)
            mean_var(5)
            tile_stats(7)
            mean_var(6)
            grid_step(4)
            mean_var(7)
            rest_h(0, 1)
            grid_clip(4)
            grid_step(5)
            for n in range(4, 8):
                norm_tile(n)
            fuse_up(0)
            grid_clip(5)
            grid_add(4)
            rest_h(1, 0)
            fuse_up(1)
            rest_h(1, 1)
            grid_add(5)
            fuse_up(2)
            subtract(5)
            fuse_up(3)
            grid_step(6)
            half_scale()
            grid_clip(6)
            fuse_up(4)
            grid_add(6)
            fuse_up(5)
            grid_step(7)
            rest_f(3)
            fuse_up(6)
            grid_clip(7)
            rest_f(4)
            rest_f(5)
            fuse_up(7)
            grid_add(7)
            fuse_up(8)
            subtract(7)
            rest_f(7)
            fuse_up(9)
            fuse_up(10)
            rest_f(9)
            scale_down(0)
            rest_f(10)
            scale_down(1)
            tile_stats(8)
            fuse_up(11)
            mean_var(8)
            tile_stats(9)
            scale_down(2)
            mean_var(9)
            norm_tile(8)
            scale_down(3)
            rotate_parts(0)
            norm_tile(9)
            rotate(0)
            rest_qk(0)
            tile_stats(NT + 2)
            scale_down(4)
            mean_var(NT + 2)
            scale_down(5)
            scale_down(6)
            norm_tile(NT + 2)
            scale_down(7)
            for c in range(NT - 1):
                rotate_parts(c + 1)
                mask_scores(c, 0)
                rotate(c + 1)
                mask_scores(c, 1)
                if c >= 2:
                    group_norm(c - 2)
                rest_qk(c + 1)
                if c >= 2:
                    gated(c - 2)
                mask_scores(c, 2)
                mask_scores(c, 3)
                if c >= 2:
                    add_proj(c - 2)
                if c + 3 < NT:
                    norm_stats(NT + c + 3, NT + c + 4)
                elif c == NT - 3:
                    norm_stats(2 * NT, 2 * NT + 2)
                elif c == NT - 2:
                    norm_stats(2 * NT + 2, 2 * NT + TH)
                if c >= 1:
                    group_mean(c - 1)
                if c + 3 < NT:
                    norm(NT + c + 3, NT + c + 4)
                copy_state(c)
                if 1 <= c < NT - 2:
                    group_var(c - 1)
            c, j0 = NT - 1, NG * NI
            mask_scores(c, 0)
            group_var(c - 2)
            norm_tile(2 * NT)
            mask_scores(c, 1)
            norm_tile(2 * NT + 1)
            mask_scores(c, 2)
            norm_tile(2 * NT + 2)
            norm_tile(2 * NT + 3)
            mask_scores(c, 3)
            group_norm(c - 2)
            rest_h(2, 0)
            rest_h(2, 1)
            group_mean(c - 1)
            gated(c - 2)
            group_var(c - 1)
            group_mean(c)
            fuse_up(j0)
            group_var(c)
            add_proj(c - 2)
            rest_f(j0)
            fuse_up(j0 + 1)
            group_norm(c - 1)
            rest_f(j0 + 1)
            fuse_up(j0 + 2)
            gated(c - 1)
            norm_stats(2 * NT + TH, 3 * NT - 2)
            rest_f(j0 + 2)
            fuse_up(j0 + 3)
            add_proj(c - 1)
            group_norm(c)
            rest_f(j0 + 3)
            fuse_up(j0 + 4)
            gated(c)
            norm_stats(3 * NT - 2, 3 * NT - 1)
            rest_f(j0 + 4)
            fuse_up(j0 + 5)
            add_proj(c)
            tile_stats(3 * NT - 1)
            norm(2 * NT + TH, 3 * NT - 2)
            mean_var(3 * NT - 1)
            norm(3 * NT - 2, 3 * NT - 1)
            rest_f(j0 + 5)
            norm(3 * NT - 1, 3 * NT)
            rest_h(3, 0)
            rest_h(3, 1)
            for d in range(NT, NT + 3):
                scale_down(d)
                add_down(d)
            for i in range(NI):
                fuse_up(j0 + NI + i)
                if i:
                    rest_f(j0 + NI + i - 1)
                if i == 1:
                    scale_down(NT + 3)
                    add_down(NT + 3)
            rest_f(j0 + 2 * NI - 1)
            for d in range(NT + TH, 2 * NT):
                scale_down(d)
                add_down(d)

        @block.tensor
        def _(pe):
            def turn_h(g):
                n0 = (g if g < NG else g + NG) * TH
                if g == 1:
                    pe.wait_ge(hlo_done, KC)
                if g == 2:
                    pe.wait_ge(qT_copied, NT)
                    pe.wait_ge(k_copied, NT)
                if g == 3:
                    pe.wait_ge(sc_masked, HG * NT)
                    pe.wait_ge(gd_done, NT)
                for t in range(TH):
                    pe.wait_ge(h_done, n0 + t + 1)
                    for k in range(KC):
                        mm = pe.transpose(turn[g][k][:, t * P:(t + 1) * P], h[:, (n0 + t) % TH, k * P:(k + 1) * P], ident)
                    mm.then_inc(turned, 1)

            def gate_up(j, parts=("gate", "up")):
                g, i = PRODUCTS[j]
                if g < NG:
                    pe.wait_ge(w_ready, PIECES_NEEDED[i])
                if i == 0:
                    pe.wait_ge(hhi_done, KC * (g + 1))
                if j >= 2:
                    pe.wait_ge(silu_done, j - 1)
                    pe.wait_ge(fuse_done, j - 1)
                if j == NG * NI:
                    pe.wait_ge(sg_done, NT)
                for m in parts:
                    dst = pairs[g // NG][j % 2][m == "up"]
                    if j == NG * NI and m == "up":
                        pe.wait_ge(yT_done, NT)
                    for half in (hhi, hlo):
                        if half is hlo:
                            pe.wait_ge(hlo_done, KC * (g + 1))
                        for k in range(KC):
                            mm = pe.matmul(dst[:, :], wr[m][:, k * I + i * P:k * I + (i + 1) * P], half[:, k, g % NG, :],
                                           start=(k == 0 and half is hhi), stop=(k == KC - 1 and half is hlo))
                    mm.then_inc(gate_done if m == "gate" else up_done, 1)

            def down(d, first=0, last=NI):
                g, t = divmod(d, TH)
                n = products_until(g, last - 1)
                pe.wait_ge(flo_dve, rests(n)[0])
                pe.wait_ge(flo_pool, rests(n)[1])
                if d == 0:
                    pe.wait_ge(w_ready, len(PIECES) - 1 if last <= NI // 2 else len(PIECES))
                if first == 0:
                    if d == 1:
                        pe.wait_ge(vec_done, 2)
                    elif 2 <= d < NT or NT + 2 <= d < NT + 6:
                        pe.wait_ge(yd_done, d - 1)
                    elif d == NT:
                        pe.wait_ge(state_done, NT - 1)
                    elif d == NT + 1:
                        pe.wait_ge(x2_done, NT)
                    elif d >= NT + 6:
                        pe.wait_ge(hlo_done, 2 * NG * KC)
                for i in range(first, last):
                    for half in (fhi, flo):
                        mm = pe.matmul(downs[d][:, 0:C], half[:, g % NG, i, t * P:(t + 1) * P],
                                       wr["down"][:, i * C:(i + 1) * C],
                                       start=(i == 0 and half is fhi), stop=(i == NI - 1 and half is flo))
                if last == NI:
                    mm.then_inc(down_done, 1)

            def turn_h2(c):
                pe.wait_ge(h_done, NT + c + 1)
                if c == 0:
                    pe.wait_ge(hlo_done, KC * NG)
                elif c == 1:
                    pe.wait_ge(h2_done, 1)
                else:
                    pe.wait_ge(q_copied, c - 1)
                for k in range(KC):
                    mm = pe.transpose(b_turn[:, k * P:(k + 1) * P], h[:, (NT + c) % TH, k * P:(k + 1) * P], ident)
                mm.then_inc(turned, 1)

            def project_qk(c):
                pe.wait_ge(h2_done, c + 1)
                if c == 0:
                    pe.wait_ge(wqkv_in, 16)
                else:
                    pe.wait_ge(k_copied, c)
                for k in range(KC):
                    mm = pe.matmul(b_qk[:, :], h2[:, c % 2, k, :], wqkv[:, k, 0:2 * C], start=(k == 0), stop=(k == KC - 1))
                mm.then_inc(qk_done, 1)

            def project_vg(c):
                if c == 0:
                    pe.wait_ge(wg_in, 16)
                    pe.wait_ge(silu_done, NG * NI)
                else:
                    pe.wait_ge(sg_done, c)
                for k in range(KC):
                    pe.matmul(b_vg[:, 0:C], h2[:, c % 2, k, :], wqkv[:, k, 2 * C:3 * C], start=(k == 0), stop=(k == KC - 1))
                for m in range(KC):
                    for k in range(KC):
                        mm = pe.matmul(b_vg[:, C + m * P:C + (m + 1) * P], wg[:, k, m * P:(m + 1) * P],
                                       h2[:, c % 2, k, :], start=(k == 0), stop=(k == KC - 1))
                mm.then_inc(vg_done, 1)

            def turn_qk(c):
                pe.wait_ge(rlo_done, c + 1)
                pe.wait_ge(rs_done, c + 1)
                pe.wait_ge(h2_done, min(c + 2, NT))
                if c >= 1:
                    pe.wait_ge(qT_copied, c)
                for dst, g0, done in ((b_qk, HG, k_turned), (b_turn, 0, q_turned)):
                    for g in range(HG):
                        mm = pe.transpose(dst[:, g * P:(g + 1) * P],
                                          rot2[:, g0 + g].rearrange("p a d -> p (a d)").bitcast(F32), ident)
                    mm.then_inc(done, 1)

            def turn_qT(c):
                pe.wait_ge(q_copied, c + 1)
                for k in range(KC):
                    mm = pe.transpose(b_turn[:, C + k * P:C + (k + 1) * P], rot[:, c % 2, k * P:(k + 1) * P], ident)
                mm.then_inc(qT_turned, 1)

            def scores(c, g):
                n = c * HG + g
                if g == 0:
                    pe.wait_ge(q_copied, c + 1)
                    pe.wait_ge(k_copied, c + 1)
                if n >= 2:
                    pe.wait_ge(sc_masked, n - 1)
                elif n == 0:
                    pe.wait_ge(fuse_done, NG * NI)
                    pe.wait_ge(silu_done, NG * NI)
                for a in range(2):
                    mm = pe.matmul(b_sc[g % 2][:, :], kk[:, c % 2, a, g, :], qM[c % 2][:, g].rearrange("p m t -> p (m t)"),
                                   start=(a == 0), stop=(a == 1))
                mm.then_inc(sc_done, 1)

            def values(c, k):
                if k == 0:
                    pe.wait_ge(v_done, c + 1)
                    if c >= 1:
                        pe.wait_ge(yT_done, c)
                if c >= 1:
                    pe.wait_ge(state_done, c)
                    pe.wait_ge(qT_copied, c + 1)
                    pe.matmul(b_y[:, k * P:(k + 1) * P], state[:, k, :], qT[:, c % 2, k, :], start=True, stop=False,
                              skip_group_check=True)
                for g in (2 * k, 2 * k + 1):
                    pe.wait_ge(sc_masked, c * HG + g + 1)
                    for m in range(HG):
                        hd = g * HG + m
                        r = (hd // 2 % 4) * 2 * D
                        mm = pe.matmul(b_y[r:r + 2 * D, k * P:(k + 1) * P], v2[:, c % 2, hd, :], sc[:, g, m, :],
                                       start=(c == 0 and hd % 2 == 0), stop=(hd % 2 == 1), skip_group_check=True)
                mm.then_inc(y_half, 1)

            def update_state(c):
                if c == 0:
                    pe.wait_ge(yd_done, NT - 1)
                else:
                    pe.wait_ge(state_done, c)
                for k in range(KC):
                    mm = pe.matmul(b_state[:, k * P:(k + 1) * P], rot[:, c % 2, C + k * P:C + (k + 1) * P],
                                   v_own[c % 2][:, 4 * k:4 * k + 4], start=(c == 0 and k == 0), stop=(k == KC - 1),
                                   skip_group_check=True)
                mm.then_inc(kv_done, 1)

            def turn_y(c):
                pe.wait_ge(yT_done, c + 1)
                if c == 0:
                    pe.wait_ge(yd_done, NT)
                elif c >= NT - 2:
                    pe.wait_ge(sc_masked, HG * NT + NT - 2 - c)
                else:
                    pe.wait_ge(x2_done, c)
                for k in range(KC):
                    mm = pe.transpose(b_turned_y[c][:, k * P:(k + 1) * P], yT[:, c % 2, k, :], ident)
                mm.then_inc(y_turned, 1)

            def turn_gn(c):
                pe.wait_ge(gn_done, c + 1)
                if c >= 1:
                    pe.wait_ge(x2_done, c)
                for k in range(KC):
                    mm = pe.transpose(b_gn[:, C + k * P:C + (k + 1) * P], gn[:, k * P:(k + 1) * P], ident)
                mm.then_inc(gn_turned, 1)

            def project_out(c):
                pe.wait_ge(go_done, c + 1)
                if c == 0:
                    pe.wait_ge(wp_in, 16)
                pe.wait_ge(gd_done, c + 1)
                pe.wait_ge(ga_done, c + 1)
                for k in range(KC):
                    mm = pe.matmul(b_gn[:, C:2 * C], go[:, k, :], wp[:, k, :], start=(k == 0), stop=(k == KC - 1))
                mm.then_inc(proj_done, 1)

            pe.wait_ge(v_zero, 1)
            zeros = v2[:, 0].rearrange("p h w -> p (h w)")
            for _ in range(WARM_UP):
                pe.matmul(bank[6][:, :], zeros[:, 0:P], zeros, start=True, stop=True)
            pe.wait_ge(mask_in, 16)
            pe.wait_ge(rows_in, 16 * 4)
            pe.transpose(bank[7][:, 0:2 * NI + 2 * KC], rows[:, :], ident[0:2 * NI + 2 * KC, 0:2 * NI + 2 * KC]).then_inc(vec_turned, 1)
            turn_h(0)
            gate_up(0)
            turn_h(1)
            for j in range(1, 9):
                gate_up(j)
            down(0, 0, NI // 2)
            down(1, 0, NI // 2)
            gate_up(9)
            gate_up(10)
            down(0, NI // 2)
            down(1, NI // 2)
            gate_up(11)
            down(2)
            down(3)
            turn_h2(0)
            down(4, 0, NI // 2)
            project_qk(0)
            down(5, 0, NI // 2)
            project_vg(0)
            turn_h2(1)
            down(4, NI // 2)
            down(5, NI // 2)
            turn_qk(0)
            down(6)
            project_qk(1)
            down(7)
            for c in range(NT - 1):
                scores(c, 0)
                if c + 2 < NT:
                    turn_h2(c + 2)
                turn_qT(c)
                scores(c, 1)
                project_vg(c + 1)
                scores(c, 2)
                scores(c, 3)
                if c >= 2:
                    turn_gn(c - 2)
                turn_qk(c + 1)
                values(c, 0)
                if c >= 2:
                    project_out(c - 2)
                values(c, 1)
                if c >= 1:
                    turn_y(c - 1)
                update_state(c)
                if c + 2 < NT:
                    project_qk(c + 2)
            c, j0 = NT - 1, NG * NI
            scores(c, 0)
            turn_qT(c)
            scores(c, 1)
            scores(c, 2)
            values(c, 0)
            scores(c, 3)
            turn_h(2)
            values(c, 1)
            turn_y(c - 1)
            turn_gn(c - 2)
            turn_y(c)
            gate_up(j0)
            project_out(c - 2)
            gate_up(j0 + 1)
            gate_up(j0 + 2)
            turn_gn(c - 1)
            gate_up(j0 + 3)
            project_out(c - 1)
            gate_up(j0 + 4)
            turn_gn(c)
            gate_up(j0 + 5)
            project_out(c)
            down(NT, 0, NI - 2)
            down(NT + 1, 0, NI - 2)
            turn_h(3)
            down(NT, NI - 2)
            down(NT + 1, NI - 2)
            gate_up(j0 + NI)
            down(NT + 2)
            gate_up(j0 + NI + 1)
            down(NT + 3)
            for j in range(j0 + NI + 2, j0 + 2 * NI):
                gate_up(j)
            d = NT + TH
            down(d, 0, NI - 2)
            for d in range(NT + TH + 1, 2 * NT):
                down(d, 0, NI - 2)
                down(d - 1, NI - 2)
            down(2 * NT - 1, NI - 2)


_INS = ["L0_attn_x", "L0_attn_w_qkv", "L0_attn_w_g", "L0_attn_w_proj", "L0_attn_gn_weight", "L0_attn_gn_bias",
        "L0_ffn_gate_w", "L0_ffn_up_w", "L0_ffn_down_w", "L0_ffn_gate_scale", "L0_ffn_up_scale", "L0_ffn_down_scale"]


def kernel(**inputs):
    import concourse.bacc as bacc
    from concourse.bass_utils import run_bass_kernel_spmd

    nc = bacc.Bacc("TRN2", target_bir_lowering=False, num_devices=1)
    given = {name: np.ascontiguousarray(inputs[name]) for name in _INS}
    given |= {"rotation": rotation_table(), "masks": masks()}
    arrays, args = {}, []
    for name, a in given.items():
        arrays[f"in_{name}"] = a
        args.append(nc.dram_tensor(f"in_{name}", a.shape, mybir.dt.from_np(a.dtype), kind="ExternalInput").ap())
    out = nc.dram_tensor("out", (1, T, C), F32, kind="ExternalOutput").ap()
    macaron(nc, *args, out)
    r = run_bass_kernel_spmd(nc, [arrays], core_ids=[0])
    return np.asarray(r.results[0]["out"])
```
